# Optimizing a Trainium2 kernel written in Bass

```python
import numpy as np
import jax
import jax.numpy as jnp

def _softmax(x, axis=-1):
    return jax.nn.softmax(x, axis=axis)

def _gelu(x):
    return jax.nn.gelu(x, approximate=True)

def _silu(x):
    return jax.nn.silu(x)

def _sigmoid(x):
    return jax.nn.sigmoid(x)

def _layernorm(x, axis=-1, eps=1e-05):
    m = jnp.mean(x, axis=axis, keepdims=True)
    v = jnp.var(x, axis=axis, keepdims=True)
    return (x - m) / jnp.sqrt(v + eps)

def _scatter_add(tgt, idx, src, axis=0):
    return tgt.at[idx].add(src)

def _segment_sum(src, seg, n):
    return jax.ops.segment_sum(src, seg, n)
kernel_name = 'mk_seq_preln_d2_jaxref_r4_fb929d'

def setup_inputs(seed: int=0):
    np.random.seed(seed)
    _w = jnp.asarray

    def _L0_attn_setup():
        import jax, jax.numpy as jnp
        import numpy as np
        N_HEAD = 16
        ROPE_BASE = 10000.0

        def _rope(Y, d_param):
            b, h, t, dh = Y.shape
            mid = d_param // 2
            Y1 = Y[:, :mid]
            Y2 = Y[:, mid:]
            Ym1 = jnp.concatenate([Y1, Y2], axis=1)
            Ym2 = jnp.concatenate([-Y2, Y1], axis=1)
            j = jnp.arange(t, dtype=Y.dtype)[:, None]
            i = jnp.arange(dh // 2, dtype=Y.dtype)[None, :]
            theta = j * jnp.power(jnp.asarray(ROPE_BASE, Y.dtype), -2.0 * i / dh)
            cos = jnp.cos(theta)
            sin = jnp.sin(theta)
            theta1 = jnp.concatenate([cos, cos], axis=1)
            theta2 = jnp.concatenate([sin, sin], axis=1)
            return Ym1 * theta1 + Ym2 * theta2
        key = jax.random.key(seed)
        ks = jax.random.split(key, 9)
        b, t, e = (2, 512, 256)
        s = 1.0 / np.sqrt(e)
        return {'x': jax.random.normal(ks[0], (b, t, e), dtype=jnp.float32), 'Wq': jax.random.normal(ks[1], (e, e), dtype=jnp.float32) * s, 'bq': jax.random.normal(ks[2], (e,), dtype=jnp.float32) * 0.01, 'Wk': jax.random.normal(ks[3], (e, e), dtype=jnp.float32) * s, 'bk': jax.random.normal(ks[4], (e,), dtype=jnp.float32) * 0.01, 'Wv': jax.random.normal(ks[5], (e, e), dtype=jnp.float32) * s, 'bv': jax.random.normal(ks[6], (e,), dtype=jnp.float32) * 0.01, 'Wo': jax.random.normal(ks[7], (e, e), dtype=jnp.float32) * s, 'bo': jax.random.normal(ks[8], (e,), dtype=jnp.float32) * 0.01}
    _L0_attn_in = _L0_attn_setup()

    def _L0_ffn_setup():
        import jax, jax.numpy as jnp
        import numpy as np
        TOP_K = 8
        key = jax.random.key(seed)
        k1, k2, k3, k4, k5 = jax.random.split(key, 5)
        B, S, D, F, E = (2, 512, 256, 192, 64)
        return {'hidden_states': jax.random.normal(k1, (B, S, D), dtype=jnp.float32), 'gate_w': jax.random.normal(k2, (E, D), dtype=jnp.float32) * 0.02, 'w_gate': jax.random.normal(k3, (E, F, D), dtype=jnp.float32) * 0.02, 'w_up': jax.random.normal(k4, (E, F, D), dtype=jnp.float32) * 0.02, 'w_down': jax.random.normal(k5, (E, D, F), dtype=jnp.float32) * 0.02}
    _L0_ffn_in = _L0_ffn_setup()

    def _L1_attn_setup():
        import jax, jax.numpy as jnp
        import numpy as np
        D_MODEL = 256
        D_STATE = 16
        D_CONV = 4
        EXPAND = 2
        D_INNER = D_MODEL * EXPAND
        B_BATCH = 2
        SEQ_L = 512
        key = jax.random.key(seed)
        ks = jax.random.split(key, 9)
        x = jax.random.normal(ks[0], (B_BATCH, SEQ_L, D_MODEL), dtype=jnp.float32)
        in_proj_w = jax.random.normal(ks[1], (2 * D_INNER, D_MODEL), jnp.float32) / np.sqrt(D_MODEL)
        conv_w = jax.random.normal(ks[2], (D_INNER, 1, D_CONV), jnp.float32) / np.sqrt(D_CONV)
        conv_b = jax.random.normal(ks[3], (D_INNER,), jnp.float32) * 0.01
        dt_w = jax.random.normal(ks[4], (D_INNER, D_INNER), jnp.float32) / np.sqrt(D_INNER)
        dt_b = jax.random.uniform(ks[5], (D_INNER,), jnp.float32, 1.0, 2.0)
        B_proj_w = jax.random.normal(ks[6], (D_STATE, D_INNER), jnp.float32) / np.sqrt(D_INNER)
        C_proj_w = jax.random.normal(ks[7], (D_STATE, D_INNER), jnp.float32) / np.sqrt(D_INNER)
        A_log = jnp.broadcast_to(jnp.log(jnp.linspace(1.0, D_STATE, D_STATE, dtype=jnp.float32))[None, :], (D_INNER, D_STATE)).copy()
        D_param = jnp.ones((D_INNER,), jnp.float32)
        out_proj_w = jax.random.normal(ks[8], (D_MODEL, D_INNER), jnp.float32) / np.sqrt(D_INNER)
        return {'x': x, 'in_proj_w': in_proj_w, 'conv_w': conv_w, 'conv_b': conv_b, 'dt_w': dt_w, 'dt_b': dt_b, 'B_proj_w': B_proj_w, 'C_proj_w': C_proj_w, 'A_log': A_log, 'D_param': D_param, 'out_proj_w': out_proj_w}
    _L1_attn_in = _L1_attn_setup()

    def _L1_ffn_setup():
        import jax, jax.numpy as jnp
        import numpy as np
        B, N, D, E, R, K = (4, 512, 256, 8, 64, 2)
        key = jax.random.key(seed)
        ks = jax.random.split(key, 5)
        scale = 0.02
        return {'x': jax.random.normal(ks[0], (B, N, D), dtype=jnp.float32), 'gate_w': jax.random.normal(ks[1], (D, E), dtype=jnp.float32) * scale, 'Wu': jax.random.normal(ks[2], (E, D, R), dtype=jnp.float32) * scale, 'Wv': jax.random.normal(ks[3], (E, D, R), dtype=jnp.float32) * scale, 'Wo': jax.random.normal(ks[4], (E, R, D), dtype=jnp.float32) * scale}
    _L1_ffn_in = _L1_ffn_setup()
    _d = {'L0_attn_x': _L0_attn_in['x'], 'L0_attn_Wq': _L0_attn_in['Wq'], 'L0_attn_bq': _L0_attn_in['bq'], 'L0_attn_Wk': _L0_attn_in['Wk'], 'L0_attn_bk': _L0_attn_in['bk'], 'L0_attn_Wv': _L0_attn_in['Wv'], 'L0_attn_bv': _L0_attn_in['bv'], 'L0_attn_Wo': _L0_attn_in['Wo'], 'L0_attn_bo': _L0_attn_in['bo'], 'L0_ffn_gate_w': _L0_ffn_in['gate_w'], 'L0_ffn_w_gate': _L0_ffn_in['w_gate'], 'L0_ffn_w_up': _L0_ffn_in['w_up'], 'L0_ffn_w_down': _L0_ffn_in['w_down'], 'L1_attn_in_proj_w': _L1_attn_in['in_proj_w'], 'L1_attn_conv_w': _L1_attn_in['conv_w'], 'L1_attn_conv_b': _L1_attn_in['conv_b'], 'L1_attn_dt_w': _L1_attn_in['dt_w'], 'L1_attn_dt_b': _L1_attn_in['dt_b'], 'L1_attn_B_proj_w': _L1_attn_in['B_proj_w'], 'L1_attn_C_proj_w': _L1_attn_in['C_proj_w'], 'L1_attn_A_log': _L1_attn_in['A_log'], 'L1_attn_D_param': _L1_attn_in['D_param'], 'L1_attn_out_proj_w': _L1_attn_in['out_proj_w'], 'L1_ffn_gate_w': _L1_ffn_in['gate_w'], 'L1_ffn_Wu': _L1_ffn_in['Wu'], 'L1_ffn_Wv': _L1_ffn_in['Wv'], 'L1_ffn_Wo': _L1_ffn_in['Wo']}
    _x0 = _d['L0_attn_x']
    _d['L0_attn_x'] = jax.random.normal(jax.random.fold_in(jax.random.key(seed), 1), (1, 4096, 256), dtype=_x0.dtype)
    del _x0
    return _d

def reference(L0_attn_x, L0_attn_Wq, L0_attn_bq, L0_attn_Wk, L0_attn_bk, L0_attn_Wv, L0_attn_bv, L0_attn_Wo, L0_attn_bo, L0_ffn_gate_w, L0_ffn_w_gate, L0_ffn_w_up, L0_ffn_w_down, L1_attn_in_proj_w, L1_attn_conv_w, L1_attn_conv_b, L1_attn_dt_w, L1_attn_dt_b, L1_attn_B_proj_w, L1_attn_C_proj_w, L1_attn_A_log, L1_attn_D_param, L1_attn_out_proj_w, L1_ffn_gate_w, L1_ffn_Wu, L1_ffn_Wv, L1_ffn_Wo):

    def _L0_attn_ref(x, Wq, bq, Wk, bk, Wv, bv, Wo, bo):
        import jax, jax.numpy as jnp
        import numpy as np
        N_HEAD = 16
        ROPE_BASE = 10000.0

        def _rope(Y, d_param):
            b, h, t, dh = Y.shape
            mid = d_param // 2
            Y1 = Y[:, :mid]
            Y2 = Y[:, mid:]
            Ym1 = jnp.concatenate([Y1, Y2], axis=1)
            Ym2 = jnp.concatenate([-Y2, Y1], axis=1)
            j = jnp.arange(t, dtype=Y.dtype)[:, None]
            i = jnp.arange(dh // 2, dtype=Y.dtype)[None, :]
            theta = j * jnp.power(jnp.asarray(ROPE_BASE, Y.dtype), -2.0 * i / dh)
            cos = jnp.cos(theta)
            sin = jnp.sin(theta)
            theta1 = jnp.concatenate([cos, cos], axis=1)
            theta2 = jnp.concatenate([sin, sin], axis=1)
            return Ym1 * theta1 + Ym2 * theta2
        b, t, e = x.shape
        h = N_HEAD
        dh = e // h

        def proj(W, bias):
            y = jnp.einsum('bte,fe->btf', x, W) + bias
            return y.reshape(b, t, h, dh).transpose(0, 2, 1, 3)
        q = _rope(proj(Wq, bq), e)
        k = _rope(proj(Wk, bk), e)
        v = proj(Wv, bv)
        scale = jnp.sqrt(jnp.asarray(dh, x.dtype))
        att = jnp.einsum('bhqd,bhkd->bhqk', q, k) / scale
        causal = jnp.tril(jnp.ones((t, t), dtype=bool))
        att = jnp.where(causal[None, None], att, -jnp.inf)
        att = jax.nn.softmax(att, axis=-1)
        y = jnp.einsum('bhqk,bhkd->bhqd', att, v)
        y = y.transpose(0, 2, 1, 3).reshape(b, t, e)
        return jnp.einsum('bte,fe->btf', y, Wo) + bo

    def _L0_ffn_ref(hidden_states, gate_w, w_gate, w_up, w_down):
        import jax, jax.numpy as jnp
        import numpy as np
        TOP_K = 8
        B, S, D = hidden_states.shape
        E = gate_w.shape[0]
        x = hidden_states.reshape(-1, D)
        logits = x.astype(jnp.float32) @ gate_w.astype(jnp.float32).T
        scores = jax.nn.softmax(logits, axis=-1)
        topk_w, topk_ids = jax.lax.top_k(scores, TOP_K)
        topk_w = topk_w / (topk_w.sum(axis=-1, keepdims=True) + 1e-20)
        flat_ids = topk_ids.reshape(-1)
        sort_idx = jnp.argsort(flat_ids)
        sorted_tokens = x[sort_idx // TOP_K]
        group_sizes = jnp.zeros((E,), jnp.int32).at[flat_ids].add(1)
        g = jax.lax.ragged_dot(sorted_tokens, jnp.swapaxes(w_gate, 1, 2), group_sizes)
        u = jax.lax.ragged_dot(sorted_tokens, jnp.swapaxes(w_up, 1, 2), group_sizes)
        h = jax.nn.silu(g) * u
        out = jax.lax.ragged_dot(h, jnp.swapaxes(w_down, 1, 2), group_sizes)
        unsorted = jnp.zeros_like(out).at[sort_idx].set(out)
        y = (unsorted.reshape(B * S, TOP_K, D) * topk_w[..., None]).sum(axis=1)
        return y.reshape(B, S, D)

    def _L1_attn_ref(x, in_proj_w, conv_w, conv_b, dt_w, dt_b, B_proj_w, C_proj_w, A_log, D_param, out_proj_w):
        import jax, jax.numpy as jnp
        import numpy as np
        D_MODEL = 256
        D_STATE = 16
        D_CONV = 4
        EXPAND = 2
        D_INNER = D_MODEL * EXPAND
        B_BATCH = 2
        SEQ_L = 512
        Bb, L, _ = x.shape
        xz = jnp.einsum('bld,ed->ble', x, in_proj_w)
        x_p, z = jnp.split(xz, 2, axis=-1)
        xc = x_p.transpose(0, 2, 1)
        K = conv_w.shape[-1]
        xc = jax.lax.conv_general_dilated(xc, conv_w, window_strides=(1,), padding=[(K - 1, 0)], feature_group_count=xc.shape[1])
        xc = xc + conv_b[None, :, None]
        xs = jax.nn.silu(xc).transpose(0, 2, 1)
        dt = jax.nn.softplus(jnp.einsum('bld,ed->ble', xs, dt_w) + dt_b)
        Bp = jnp.einsum('bld,nd->bln', xs, B_proj_w)
        Cp = jnp.einsum('bld,nd->bln', xs, C_proj_w)
        A = -jnp.exp(A_log)

        def step(h, inp):
            dt_t, B_t, x_t, C_t = inp
            a = jnp.exp(dt_t[..., None] * A)
            b = dt_t[..., None] * B_t[:, None, :] * x_t[..., None]
            h = a * h + b
            y_t = jnp.einsum('bdn,bn->bd', h, C_t)
            return (h, y_t)
        h0 = jnp.zeros((Bb, xs.shape[-1], A.shape[1]), x.dtype)
        scan_in = (dt.transpose(1, 0, 2), Bp.transpose(1, 0, 2), xs.transpose(1, 0, 2), Cp.transpose(1, 0, 2))
        _, ys = jax.lax.scan(step, h0, scan_in)
        y = ys.transpose(1, 0, 2) + D_param * xs
        y = y * jax.nn.silu(z)
        return jnp.einsum('ble,de->bld', y, out_proj_w)

    def _L1_ffn_ref(x, gate_w, Wu, Wv, Wo):
        import jax, jax.numpy as jnp
        import numpy as np
        B, N, D, E, R, K = (4, 512, 256, 8, 64, 2)
        logits = jnp.einsum('bnd,de->bne', x, gate_w)
        topv, topi = jax.lax.top_k(logits, K)
        w = jax.nn.softmax(topv, axis=-1)
        u = jnp.einsum('bnd,edr->bner', x, Wu)
        v = jnp.einsum('bnd,edr->bner', x, Wv)
        s = jax.nn.silu(u) * v
        Y = jnp.einsum('bner,erd->bned', s, Wo)
        y_sel = jnp.take_along_axis(Y, topi[..., None], axis=2)
        out = jnp.einsum('bnkd,bnk->bnd', y_sel, w)
        return out
    x = L0_attn_x
    x = x + _L0_attn_ref(_layernorm(x, axis=-1), L0_attn_Wq, L0_attn_bq, L0_attn_Wk, L0_attn_bk, L0_attn_Wv, L0_attn_bv, L0_attn_Wo, L0_attn_bo)
    x = x + _L0_ffn_ref(_layernorm(x, axis=-1), L0_ffn_gate_w, L0_ffn_w_gate, L0_ffn_w_up, L0_ffn_w_down)
    x = x + _L1_attn_ref(_layernorm(x, axis=-1), L1_attn_in_proj_w, L1_attn_conv_w, L1_attn_conv_b, L1_attn_dt_w, L1_attn_dt_b, L1_attn_B_proj_w, L1_attn_C_proj_w, L1_attn_A_log, L1_attn_D_param, L1_attn_out_proj_w)
    x = x + _L1_ffn_ref(_layernorm(x, axis=-1), L1_ffn_gate_w, L1_ffn_Wu, L1_ffn_Wv, L1_ffn_Wo)
    return x

_drawn_inputs = setup_inputs


def setup_inputs(seed=0):
    import zlib

    import numpy as np

    out = dict(_drawn_inputs(seed))
    spreads = {'L1_attn_D_param': (1.0, 0.2)}
    factors = {'L0_attn_bq': 8.0,
     'L0_attn_bk': 8.0,
     'L0_attn_bv': 3.136,
     'L0_attn_bo': 3.933,
     'L0_ffn_gate_w': 6.832,
     'L0_ffn_w_gate': 6.439,
     'L0_ffn_w_up': 6.198,
     'L0_ffn_w_down': 6.277,
     'L1_attn_conv_b': 4.612,
     'L1_ffn_gate_w': 8.0,
     'L1_ffn_Wu': 8.0,
     'L1_ffn_Wv': 8.0,
     'L1_ffn_Wo': 8.0}
    for name, (base, spread) in spreads.items():
        noise = np.random.default_rng([zlib.crc32(name.encode()), seed]).standard_normal(out[name].shape)
        drawn = base * np.exp(spread * noise) if base else spread * noise
        out[name] = jnp.asarray(drawn.astype(out[name].dtype))
    for name, factor in factors.items():
        out[name] = (out[name] * factor).astype(out[name].dtype)
    return out
```

```python
from contextlib import ExitStack

import numpy as np

import concourse.bass as bass
from concourse import mybir
from concourse.alu_op_type import AluOpType as ALU

F32 = mybir.dt.float32
BF16 = mybir.dt.bfloat16
I32 = mybir.dt.int32
U32 = mybir.dt.uint32
ACT = mybir.ActivationFunctionType
AX_X = mybir.AxisListType.X

P = 128
T = 4096
D = 256
KD = D // P
CH = 512
NCH = T // CH
TT = T // P
HEADS, DH = 16, 16
NEG = -1.0e30
EXPERTS, TOPK, FF = 64, 8, 192
SLOT_TILE = 256
SLOT_TILES = (T * TOPK + EXPERTS * (SLOT_TILE - 1)) // SLOT_TILE
SLOT_TILES += -SLOT_TILES % 4
SLOTS = SLOT_TILES * SLOT_TILE
DI, NS, TAPS = 512, 16, 4
KI = DI // P
BC = 3 * 2 * NS
E2, R2 = 8, 64
KR = E2 * R2 // P
EPS = 1e-5


def ds(start, size):
    return bass.ds(start, size)


class Stage:

    def __init__(self, nc, name):
        self.nc, self.name, self.ctx, self.sems = nc, name, ExitStack(), []

    def __enter__(self):
        return self

    def __exit__(self, *a):
        self.nc.clear_and_free_semaphores(self.sems)
        self.nc.all_engine_barrier()
        self.ctx.close()

    def sb(self, name, shape, dt=F32):
        return self.ctx.enter_context(self.nc.sbuf_tensor(f"{self.name}_{name}", shape, dt))

    def ps(self, name, shape, dt=F32):
        return self.ctx.enter_context(self.nc.psum_tensor(f"{self.name}_{name}", shape, dt))

    def sem(self, name):
        self.sems.append(self.nc.alloc_semaphore(f"{self.name}_{name}"))
        return self.sems[-1]

    def block(self):
        return self.nc.Block()


def layernorm(nc, name, w, x_t, y_t, x_dram=None):
    G = 4
    with Stage(nc, name) as s:
        ones = s.sb("ones", [P, P])
        eps = s.sb("eps", [P, 1])
        to_row = s.sb("to_row", [P, G, G])
        pick = s.sb("pick", [G, G, P])
        sq = s.sb("sq", [P, KD, T])
        std = s.sb("std", [G, 2, CH])
        rstd = s.sb("rstd", [G, 2, CH])
        mean = s.ps("mean", [P, 2, CH])
        var = s.ps("var", [P, 2, CH])
        scale = s.ps("scale", [P, 2, CH])
        loaded = s.sem("loaded")
        x_loaded = [s.sem(f"x_loaded{c}") for c in range(NCH if x_dram is not None else 0)]
        const_ready = s.sem("const_ready")
        mean_ready = s.sem("mean_ready")
        centered = s.sem("centered")
        squared = s.sem("squared")
        var_ready = s.sem("var_ready")
        std_ready = s.sem("std_ready")
        rstd_ready = s.sem("rstd_ready")
        spread = s.sem("spread")
        normed = s.sem("normed")
        with s.block() as block:
            @block.sync
            def _(sp):
                if x_dram is not None:
                    for c in range(NCH):
                        cols = slice(c * CH, (c + 1) * CH)
                        sp.dma_start(x_t[:, :, cols], x_dram[:, :, cols]).then_inc(x_loaded[c], 16)
                sp.dma_start(to_row[:], w["to_row"]).then_inc(loaded, 16)
                sp.dma_start(pick[:], w["pick"]).then_inc(loaded, 16)

            @block.gpsimd
            def _(pool):
                pool.memset(ones[:], 1.0 / D).then_inc(const_ready, 1)
                pool.memset(eps[:], EPS).then_inc(const_ready, 1)

            @block.tensor
            def _(pe):
                pe.wait_ge(const_ready, 2)
                for c in range(NCH):
                    pe.wait_ge(centered, c + 1)
                    if x_dram is not None:
                        pe.wait_ge(x_loaded[c], 16)
                    for k in range(KD):
                        mm = pe.matmul(mean[:, c % 2, :], ones[:], x_t[:, k, c * CH:(c + 1) * CH],
                                       start=(k == 0), stop=(k == KD - 1))
                    mm.then_inc(mean_ready, 1)
                pe.wait_ge(loaded, 32)
                for c in range(NCH):
                    pe.wait_ge(squared, c + 1)
                    for k in range(KD):
                        mm = pe.matmul(var[0:G, c // G, :], to_row[:, c % G, :], sq[:, k, c * CH:(c + 1) * CH],
                                       start=(c % G == 0 and k == 0), stop=(c % G == G - 1 and k == KD - 1))
                    if c % G == G - 1:
                        mm.then_inc(var_ready, 1)
                for c in range(NCH):
                    pe.wait_ge(rstd_ready, c // G + 1)
                    if c >= 2:
                        pe.wait_ge(normed, c - 1)
                    pe.matmul(scale[:, c % 2, :], pick[:, c % G, :], rstd[:, c // G, :], start=True,
                              stop=True).then_inc(spread, 1)

            @block.vector
            def _(dve):
                dve.nop().then_inc(centered, 2)
                with dve.Fori(0, NCH // 2) as pair:
                    i = pair * 2
                    for u in range(2):
                        dve.wait_ge(mean_ready, i + (u + 1))
                        for k in range(KD):
                            c = ds(i * CH + u * CH, CH)
                            tt = dve.tensor_tensor(y_t[:, k, c], x_t[:, k, c], mean[:, u, :], ALU.subtract)
                        tt.then_inc(centered, 1)
                for g in range(NCH // G):
                    dve.wait_ge(std_ready, g + 1)
                    dve.reciprocal(rstd[:, g, :], std[:, g, :]).then_inc(rstd_ready, 1)
                for c in range(NCH):
                    dve.wait_ge(spread, c + 1)
                    y_c = y_t[:, :, c * CH:(c + 1) * CH]
                    dve.tensor_tensor(y_c, y_c, scale[:, c % 2, :].unsqueeze(1).to_broadcast([P, KD, CH]),
                                      ALU.mult).then_inc(normed, 1)

            @block.scalar
            def _(act):
                with act.Fori(0, NCH) as c:
                    act.wait_ge(centered, c + 3)
                    act.activation(sq[:, :, ds(c * CH, CH)], y_t[:, :, ds(c * CH, CH)], ACT.Square).then_inc(squared, 1)
                act.wait_ge(const_ready, 2)
                for g in range(NCH // G):
                    act.wait_ge(var_ready, g + 1)
                    act.activation(std[:, g, :], var[0:G, g, :], ACT.Sqrt, bias=eps[0:G]).then_inc(std_ready, 1)


def project_qk(nc, xn, w, parts_dram):
    with Stage(nc, "qkv") as s:
        w_qk = s.sb("w_qk", [P, 2, KD, D])
        b_qk = s.sb("b_qk", [P, 2, KD])
        rope = s.sb("rope", [P, T])
        val = s.sb("val", [P, 4, CH])
        rest = s.sb("rest", [P, 4, CH])
        part = s.sb("part", [P, 4, 3, CH], BF16)
        ps = s.ps("ps", [P, 2, CH])
        loaded = s.sem("loaded")
        rope_loaded = s.sem("rope_loaded")
        ps_ready = s.sem("ps_ready")
        val_ready = s.sem("val_ready")
        high_ready = s.sem("high_ready")
        rest_ready = s.sem("rest_ready")
        mid_ready = s.sem("mid_ready")
        low_ready = s.sem("low_ready")
        stored = [s.sem(f"stored{j}") for j in range(4)]
        sp_passed = s.sem("sp_passed")
        steps = [(w_, m) for w_ in range(2) for m in range(KD)]
        with s.block() as block:
            @block.sync
            def _(sp):
                sp.dma_start(w_qk[:, 0], w["wq"]).then_inc(loaded, 16)
                sp.dma_start(w_qk[:, 1], w["wk"]).then_inc(loaded, 16)
                sp.dma_start(b_qk[:, 0], w["bq"]).then_inc(loaded, 16)
                sp.dma_start(b_qk[:, 1], w["bk"]).then_inc(loaded, 16)
                sp.dma_start(rope[:], w["rope"]).then_inc(rope_loaded, 16)
                for j in range(4):
                    sp.nop().then_inc(stored[j], 16)
                with sp.Fori(0, NCH) as c:
                    for j, (which, m) in enumerate(steps):
                        sp.wait_ge(low_ready, c * 4 + (j + 5))
                        sp.nop().then_inc(sp_passed, 1)
                        sp.dma_start(parts_dram[which, :, m * P:(m + 1) * P, ds(c * CH, CH)].rearrange("a p t -> p a t"),
                                     part[:, j]).then_inc(stored[j], 16)
                for j in range(4):
                    sp.wait_ge(stored[j], 16 * (NCH + 1))

            @block.gpsimd
            def _(pool):
                pool.nop().then_inc(low_ready, 4)
                with pool.Fori(0, NCH) as c:
                    for j in range(4):
                        pool.wait_ge(mid_ready, c * 4 + (j + 1))
                        pool.tensor_tensor(part[:, j, 2, :], rest[:, j, :], part[:, j, 1, :],
                                           ALU.subtract).then_inc(low_ready, 1)

            @block.tensor
            def _(pe):
                pe.wait_ge(loaded, 16 * 4)
                with pe.Fori(0, NCH) as c:
                    for j, (which, m) in enumerate(steps):
                        pe.wait_ge(val_ready, c * 4 + (j + 1))
                        for k in range(KD):
                            mm = pe.matmul(ps[:, j % 2, :], w_qk[:, which, k, m * P:(m + 1) * P],
                                           xn[:, k, ds(c * CH, CH)], start=(k == 0), stop=(k == KD - 1))
                        mm.then_inc(ps_ready, 1)

            @block.vector
            def _(dve):
                dve.nop().then_inc(val_ready, 2)
                dve.nop().then_inc(rest_ready, 4)
                dve.wait_ge(loaded, 16 * 4)
                dve.wait_ge(rope_loaded, 16)

                def value(c, j):
                    which, m = steps[j]
                    dve.wait_ge(ps_ready, c * 4 + (j + 1))
                    dve.wait_ge(rest_ready, c * 4 + (j + 1))
                    dve.scalar_tensor_tensor(out=val[:, j, :], in0=ps[:, j % 2, :], scalar=b_qk[:, which, m:m + 1],
                                             in1=rope[:, ds(c * CH, CH)], op0=ALU.add, op1=ALU.mult).then_inc(val_ready, 1)

                def less_high(c, j):
                    dve.wait_ge(high_ready, c * 4 + (j + 1))
                    dve.wait_ge(low_ready, c * 4 + (j + 1))
                    dve.tensor_tensor(rest[:, j, :], val[:, j, :], part[:, j, 0, :], ALU.subtract).then_inc(rest_ready, 1)

                value(0, 0)
                for j in range(1, 4):
                    value(0, j)
                    less_high(0, j - 1)
                with dve.Fori(1, NCH) as c:
                    for j in range(4):
                        value(c, j)
                        less_high(c if j else c - 1, (j - 1) % 4)
                less_high(NCH - 1, 3)

            @block.scalar
            def _(act):
                def high(c, j):
                    act.wait_ge(val_ready, c * 4 + (j + 3))
                    act.wait_ge(stored[j], c * 16 + 16)
                    act.activation(part[:, j, 0, :], val[:, j, :], ACT.Copy).then_inc(high_ready, 1)

                def middle(c, j):
                    act.wait_ge(rest_ready, c * 4 + (j + 5))
                    act.activation(part[:, j, 1, :], rest[:, j, :], ACT.Copy).then_inc(mid_ready, 1)

                high(0, 0)
                for j in range(1, 4):
                    high(0, j)
                    middle(0, j - 1)
                with act.Fori(1, NCH) as c:
                    for j in range(4):
                        high(c, j)
                        middle(c if j else c - 1, (j - 1) % 4)
                middle(NCH - 1, 3)


ZERO_DMAS = 3
assert SLOTS % (HEADS * ZERO_DMAS * P) == 0
PAIRS = [(0, 0), (0, 1), (0, 2), (1, 0), (1, 1), (2, 0)]
ROWS = len(PAIRS) * DH
Q_RUNS = [(0, 3, 0), (3, 2, 1), (5, 1, 2)]
K_RUNS = [(0, 3), (3, 2), (5, 1)]


def attention(nc, w, xn, parts_dram, v_all, num_dram, den_dram, xs_dram):
    ZERO_AT = 8
    EARLY = T // 4
    ZERO_ROWS = SLOTS // (HEADS * ZERO_DMAS)
    GROUPS, QUADS = 72, 36
    CHUNKS = sum(i // 4 + 1 for i in range(TT))
    quads = [(j, 4 * m) for j in range(NCH) for m in range(j + 1)]
    max_chunks = [(i, c) for i in range(TT) for c in range(i // 4 + 1)]
    per_quad, left = [], CHUNKS
    for q in range(QUADS):
        n = 0 if q < 2 else min(5 if q % 4 else 4, left)
        per_quad.append(n)
        left -= n
    assert left == 0
    max_turn = max(q for q in range(QUADS) if per_quad[q]) + 1
    with Stage(nc, "attn") as s:
        q_rows = s.sb("q_rows", [P, 2, T], BF16)
        k_rows = s.sb("k_rows", [P, 2, T], BF16)
        v_h = s.sb("v_h", [P, 2, TT, 32])
        prob = s.sb("prob", [P, 6, 2, CH])
        part_max = s.sb("part_max", [P, TT, NCH])
        neg_max = s.sb("neg_max", [P, TT])
        nm = s.sb("nm", [TT, 3, P])
        nm_part = s.sb("nm_part", [TT, 3, P], BF16)
        acc_sb = s.sb("acc_sb", [P, 2, CH])
        cst = s.sb("cst", [P, 2 * P + CH])
        ident_bf = s.sb("ident_bf", [P, P], BF16)
        mask_q = s.sb("mask_q", [P, P], BF16)
        mask_k = s.sb("mask_k", [P, CH], BF16)
        zeros = s.sb("zeros", [P, ZERO_ROWS * D // P])
        w_v = s.sb("w_v", [P, KD, D])
        b_v = s.sb("b_v", [P, D])
        ident = cst[:, 0:P]
        score = s.ps("score", [P, 2, 2, CH])
        score_q = s.ps("score_q", [P, 3, CH])
        acc = s.ps("acc", [P, CH])

        const_loaded = s.sem("const_loaded")
        wv_loaded = s.sem("wv_loaded")
        xv_ready = s.sem("xv_ready")
        v_done = s.sem("v_done")
        const_ready = s.sem("const_ready")
        early_loaded = [s.sem(f"early_loaded{u}") for u in range(2)]
        rows_loaded = [s.sem(f"rows_loaded{u}") for u in range(2)]
        v_ready = s.sem("v_ready")
        score_ready = s.sem("score_ready")
        prob_ready = s.sem("prob_ready")
        pv_done = s.sem("pv_done")
        acc_copied = s.sem("acc_copied")
        acc_stored = [s.sem(f"acc_stored{u}") for u in range(2)]
        max_scores = s.sem("max_scores")
        max_taken = s.sem("max_taken")
        neg_ready = s.sem("neg_ready")
        chain = s.sem("chain")
        turned = s.sem("turned")
        turn_copied = s.sem("turn_copied")
        nm_ready = s.sem("nm_ready")
        max_loaded = s.sem("max_loaded")
        zeroed = s.sem("zeroed")
        sp_passed = s.sem("sp_passed")

        def load_rows(sp, h, u):
            for cols, landed in ((slice(0, EARLY), early_loaded[u]), (slice(EARLY, T), rows_loaded[u])):
                width = cols.stop - cols.start
                for first, n, a in Q_RUNS:
                    sp.dma_start(q_rows[first * DH:(first + n) * DH, u, cols],
                                 parts_dram[0, a:a + 1, ds(h * DH, DH), cols].to_broadcast([n, DH, width])
                                 ).then_inc(landed, 16)
                for first, n in K_RUNS:
                    sp.dma_start(k_rows[first * DH:(first + n) * DH, u, cols],
                                 parts_dram[1, 0:n, ds(h * DH, DH), cols]).then_inc(landed, 16)

        def load_max(sp, h, u):
            sp.wait_ge(nm_ready, h + 1)
            sp.nop().then_inc(sp_passed, 1)
            for a in range(3):
                row = q_rows[ROWS + a:ROWS + a + 1, u, :].rearrange("o (i q) -> o i q", i=TT)
                sp.dma_start(row, nm_part[:, a, :]).then_inc(max_loaded, 16)

        def rows_count(h, u):
            per_head = 16 * (len(Q_RUNS) + len(K_RUNS))
            return (h - u) * (per_head // 2) + per_head

        def maximum_chunk(pe, h, u, n):
            i, c = max_chunks[n]
            width = min(CH, (i + 1) * P - c * CH)
            if n == 0:
                pe.wait_ge(early_loaded[u], rows_count(h, u))
                pe.wait_ge(turn_copied, h + 1)
            if (i, c) == (EARLY // P, 0):
                pe.wait_ge(rows_loaded[u], rows_count(h, u))
            pe.wait_ge(max_taken, h * CHUNKS + (n + 1))
            diag = c == i // 4
            free = width - P if diag else width
            lhs = q_rows[0:ROWS, u, i * P:(i + 1) * P]
            if diag:
                masked = score_q[:, n % 3, free:width]
                pe.matmul(masked, ident_bf[:], mask_q[:], start=True, stop=False)
                mm = pe.matmul(masked, lhs, k_rows[0:ROWS, u, c * CH + free:c * CH + width], start=False, stop=True)
            if free:
                mm = pe.matmul(score_q[:, n % 3, 0:free], lhs, k_rows[0:ROWS, u, c * CH:c * CH + free],
                               start=True, stop=True)
            mm.then_inc(max_scores, 1)

        def take_chunk(dve, h, n):
            i, c = max_chunks[n]
            width = min(CH, (i + 1) * P - c * CH)
            dve.wait_ge(max_scores, h * CHUNKS + (n + 1))
            dve.tensor_reduce(part_max[:, i, c:c + 1], score_q[:, n % 3, 0:width], AX_X, ALU.max).then_inc(max_taken, 1)

        V_EVERY = CHUNKS // TT

        def times_wv(pe, i):
            pe.wait_ge(v_done, i + 1)
            for k in range(KD):
                mm = pe.matmul(acc[:, 0:D], xn[:, k, i * P:(i + 1) * P], w_v[:, k, :],
                               start=(k == 0), stop=(k == KD - 1))
            mm.then_inc(xv_ready, 1)

        def add_bias(dve, i):
            dve.wait_ge(xv_ready, i + 1)
            dve.tensor_tensor(v_all[:, :, i, :], acc[:, 0:D].rearrange("p (h d) -> p h d", h=HEADS),
                              b_v[:].rearrange("p (h d) -> p h d", h=HEADS), ALU.add).then_inc(v_done, 1)

        def turn_max(pe, h):
            pe.wait_ge(neg_ready, h + 1)
            pe.transpose(score_q[0:TT, 0, 0:P], neg_max[:], ident).then_inc(turned, 1)

        def reduce_max(dve, h):
            dve.wait_ge(max_taken, h * CHUNKS + (CHUNKS + 3))
            dve.tensor_reduce(neg_max[:], part_max[:], AX_X, ALU.max, negate=True).then_inc(neg_ready, 1)

        def split_max(dve, h):
            dve.wait_ge(turned, h + 1)
            dve.tensor_copy(nm[:, 0, :], score_q[0:TT, 0, 0:P]).then_inc(turn_copied, 1)
            dve.wait_ge(turn_copied, h + 2)
            dve.wait_ge(max_loaded, h * 48 + 48)
            dve.tensor_copy(nm_part[:, 0, :], nm[:, 0, :]).then_inc(chain, 1)
            dve.wait_ge(chain, h * 4 + 1)
            dve.tensor_tensor(nm[:, 1, :], nm[:, 0, :], nm_part[:, 0, :], ALU.subtract).then_inc(chain, 1)
            dve.wait_ge(chain, h * 4 + 2)
            dve.tensor_copy(nm_part[:, 1, :], nm[:, 1, :]).then_inc(chain, 1)
            dve.wait_ge(chain, h * 4 + 3)
            dve.tensor_tensor(nm_part[:, 2, :], nm[:, 1, :], nm_part[:, 1, :], ALU.subtract).then_inc(chain, 1)
            dve.wait_ge(chain, h * 4 + 4)
            dve.nop().then_inc(nm_ready, 1)

        def first_col(j, kt):
            r = kt - 4 * j
            return 0 if r < 0 or j == 0 else (r // 2) * 2 * P

        def scores(pe, h, u, q, r):
            j, kt0 = quads[q]
            g, a = 2 * q + r // 2, r % 2
            kt = kt0 + r
            if a == 0:
                pe.wait_ge(prob_ready, h * GROUPS + (g + 1))
            lo = first_col(j, kt)
            diag = kt >= 4 * j
            hi = P * (kt - 4 * j + 1) if diag else lo
            lhs = k_rows[0:ROWS + 3, u, kt * P:(kt + 1) * P]
            if diag:
                masked = score[:, g % 2, a, lo:hi]
                pe.matmul(masked, ident_bf[:], mask_k[:, CH - hi + lo:CH], start=True, stop=False)
                mm = pe.matmul(masked, lhs, q_rows[0:ROWS + 3, u, j * CH + lo:j * CH + hi], start=False, stop=True)
            if hi < CH:
                mm = pe.matmul(score[:, g % 2, a, hi:CH], lhs, q_rows[0:ROWS + 3, u, j * CH + hi:(j + 1) * CH],
                               start=True, stop=True)
            if a == 1:
                mm.then_inc(score_ready, 1)

        def exponential(act, h, g):
            j, kt0 = quads[g // 2]
            lo = first_col(j, kt0 + 2 * (g % 2))
            act.wait_ge(score_ready, h * GROUPS + (g + 1))
            act.wait_ge(pv_done, h * QUADS + (g // 2 + 1))
            act.activation(prob[:, g % 6, :, lo:CH], score[:, g % 2, :, lo:CH], ACT.Exp,
                           scale=DH ** -0.5).then_inc(prob_ready, 1)

        def times_v(pe, h, u, q, half):
            j, kt0 = quads[q]
            starts = kt0 == 0
            if half == 0:
                if q == 0:
                    pe.wait_ge(v_ready, h + 1)
                if starts:
                    pe.wait_ge(acc_copied, h * NCH + (j + 1))
                pe.wait_ge(prob_ready, h * GROUPS + (2 * q + 4))
            elif starts:
                return
            for r in range(4):
                lo = max(first_col(j, kt0 + r), half * (CH // 2))
                hi = CH if starts else (half + 1) * (CH // 2)
                if lo < hi:
                    g = 2 * q + r // 2
                    mm = pe.matmul(acc[32 * r:32 * r + 32, lo:hi], v_h[:, u, kt0 + r, :], prob[:, g % 6, r % 2, lo:hi],
                                   start=starts, stop=(kt0 == 4 * j), skip_group_check=True)
            if starts or half == 1:
                mm.then_inc(pv_done, 1)

        def closes(q):
            if 0 <= q < QUADS and quads[q][1] == 4 * quads[q][0]:
                return quads[q][0]
            return None

        def copy_acc(act, h, j):
            act.wait_ge(pv_done, h * QUADS + (max(q for q in range(QUADS) if quads[q][0] == j) + 4))
            act.wait_ge(acc_stored[j % 2], h * (40 * NCH) + 80 * (j // 2) + 80)
            act.activation(acc_sb[:, j % 2, :], acc[:], ACT.Copy).then_inc(acc_copied, 1)

        def store_acc(sp, h, j):
            sp.wait_ge(acc_copied, h * NCH + (j + 2))
            sp.nop().then_inc(sp_passed, 1)
            cols = slice(j * CH, (j + 1) * CH)
            for g in range(4):
                sp.dma_start(num_dram[g, ds(h * DH, DH), cols],
                             acc_sb[32 * g:32 * g + DH, j % 2, :]).then_inc(acc_stored[j % 2], 16)
            sp.dma_start(den_dram[:, ds(h, 1), cols].rearrange("g o t -> g (o t)"),
                         acc_sb[DH::32, j % 2, :]).then_inc(acc_stored[j % 2], 16)

        def pe_head(pe, h, u, more):
            for q in range(QUADS + 1):
                todo = list(range(sum(per_quad[:q]), sum(per_quad[:q + 1]))) if more and q < QUADS else []

                def next_max(n=1):
                    for _ in range(min(n, len(todo))):
                        maximum_chunk(pe, h + 1, 1 - u, todo.pop(0))

                if q < QUADS:
                    if q == 0:
                        pe.wait_ge(max_loaded, h * 48 + 96)
                        pe.wait_ge(early_loaded[u], rows_count(h, u))
                        pe.wait_ge(rows_loaded[u], rows_count(h, u))
                    scores(pe, h, u, q, 0)
                    next_max()
                    scores(pe, h, u, q, 1)
                    scores(pe, h, u, q, 2)
                    next_max()
                    scores(pe, h, u, q, 3)
                    next_max()
                if 1 <= q <= QUADS:
                    times_v(pe, h, u, q - 1, 0)
                    next_max()
                    times_v(pe, h, u, q - 1, 1)
                next_max(len(todo))
                if q == max_turn and more:
                    turn_max(pe, h + 1)

        def dve_head(dve, h):
            for n in range(CHUNKS):
                take_chunk(dve, h + 1, n)
            reduce_max(dve, h + 1)
            split_max(dve, h + 1)

        def act_head(act, h):
            for q in range(QUADS + 1):
                if ZERO_AT <= q < ZERO_AT + ZERO_DMAS:
                    first_row = h * (ZERO_DMAS * ZERO_ROWS) + (q - ZERO_AT) * ZERO_ROWS
                    act.dma_start(xs_dram[ds(first_row, ZERO_ROWS), :].rearrange("(p r) d -> p (r d)", p=P),
                                  zeros[:]).then_inc(zeroed, 16)
                if q < QUADS:
                    exponential(act, h, 2 * q)
                    exponential(act, h, 2 * q + 1)
                if closes(q - 1) is not None:
                    copy_acc(act, h, closes(q - 1))

        def sp_head(sp, h, u, first, more):
            if more:
                sp.wait_ge(pv_done, h * QUADS + 2)
                sp.nop().then_inc(sp_passed, 1)
                load_rows(sp, h + 1, 1 - u)
            if not first:
                store_acc(sp, h - 1, NCH - 1)
            for j in range(NCH - 1):
                store_acc(sp, h, j)
            if more:
                load_max(sp, h + 1, 1 - u)
            else:
                store_acc(sp, h, NCH - 1)

        def pool_head(pool, h, u, more):
            if more:
                pool.wait_ge(pv_done, h * QUADS + 3)
                pool.tensor_copy(v_h[:, 1 - u, :, 0:DH],
                                 v_all[:, ds(h + 1, 1), :, :].rearrange("p o i d -> p (o i) d")).then_inc(v_ready, 1)
        with s.block() as block:
            @block.sync
            def _(sp):
                sp.nop().then_inc(acc_stored[0], 80)
                sp.nop().then_inc(acc_stored[1], 80)
                sp.nop().then_inc(max_loaded, 48)
                sp.dma_start(cst[:], w["consts"]).then_inc(const_loaded, 16)
                sp.dma_start(w_v[:], w["wv"]).then_inc(wv_loaded, 16)
                sp.dma_start(b_v[:], w["bv"]).then_inc(wv_loaded, 16)
                load_rows(sp, 0, 0)
                load_max(sp, 0, 0)
                sp_head(sp, 0, 0, True, True)
                sp_head(sp, 1, 1, False, True)
                with sp.Fori(1, HEADS // 2 - 1) as pair:
                    h = pair * 2
                    sp_head(sp, h, 0, False, True)
                    sp_head(sp, h + 1, 1, False, True)
                sp_head(sp, HEADS - 2, 0, False, True)
                sp_head(sp, HEADS - 1, 1, False, False)
                for u in range(2):
                    sp.wait_ge(acc_stored[u], 40 * NCH * HEADS + 80)

            @block.gpsimd
            def _(pool):
                pool.memset(v_h[:, :, :, DH:32], 0.0).then_inc(const_ready, 1)
                pool.memset(part_max[:], -3.0e38).then_inc(const_ready, 1)
                pool.memset(zeros[:], 0.0).then_inc(const_ready, 1)
                pool.wait_ge(const_ready, 7)
                pool.memset(v_h[:, :, :, DH:DH + 1], 1.0).then_inc(const_ready, 1)
                pool.wait_ge(v_done, TT + 1)
                pool.tensor_copy(v_h[:, 0, :, 0:DH], v_all[:, 0, :, :]).then_inc(v_ready, 1)
                with pool.Fori(0, HEADS // 2 - 1) as pair:
                    h = pair * 2
                    pool_head(pool, h, 0, True)
                    pool_head(pool, h + 1, 1, True)
                pool_head(pool, HEADS - 2, 0, True)

            @block.vector
            def _(dve):
                dve.nop().then_inc(max_taken, 3)
                dve.nop().then_inc(v_done, 1)
                dve.nop().then_inc(turn_copied, 1)
                dve.memset(k_rows[ROWS:P, :, :], 1.0).then_inc(const_ready, 1)
                dve.wait_ge(const_loaded, 16)
                dve.tensor_copy(ident_bf[:], ident).then_inc(const_ready, 1)
                dve.tensor_copy(mask_q[:], cst[:, P:2 * P]).then_inc(const_ready, 1)
                dve.tensor_copy(mask_k[:], cst[:, 2 * P:2 * P + CH]).then_inc(const_ready, 1)
                dve.wait_ge(const_ready, 8)
                dve.wait_ge(wv_loaded, 32)
                for n in range(CHUNKS):
                    take_chunk(dve, 0, n)
                    if n % V_EVERY == V_EVERY - 1 and n // V_EVERY < TT:
                        add_bias(dve, n // V_EVERY)
                reduce_max(dve, 0)
                split_max(dve, 0)
                with dve.Fori(0, HEADS // 2 - 1) as pair:
                    h = pair * 2
                    dve_head(dve, h)
                    dve_head(dve, h + 1)
                dve_head(dve, HEADS - 2)

            @block.scalar
            def _(act):
                act.nop().then_inc(prob_ready, 2)
                act.nop().then_inc(acc_copied, 1)
                act.wait_ge(const_ready, 8)
                with act.Fori(0, HEADS // 2) as pair:
                    h = pair * 2
                    act_head(act, h)
                    act_head(act, h + 1)
                act.wait_ge(zeroed, 16 * HEADS * ZERO_DMAS)

            @block.tensor
            def _(pe):
                pe.nop().then_inc(pv_done, 3)
                pe.wait_ge(const_ready, 8)
                pe.wait_ge(wv_loaded, 32)
                for n in range(CHUNKS):
                    maximum_chunk(pe, 0, 0, n)
                    if n % V_EVERY == V_EVERY - 1 and n // V_EVERY < TT:
                        times_wv(pe, n // V_EVERY)
                turn_max(pe, 0)
                pe.wait_ge(v_done, TT + 1)
                with pe.Fori(0, HEADS // 2 - 1) as pair:
                    h = pair * 2
                    pe_head(pe, h, 0, True)
                    pe_head(pe, h + 1, 1, True)
                pe_head(pe, HEADS - 2, 0, True)
                pe_head(pe, HEADS - 1, 1, False)


def attention_out(nc, w, num_dram, den_dram, x_t):
    with Stage(nc, "aout") as s:
        num = s.sb("num", [P, 2, 4, KD, CH])
        den = s.sb("den", [P, 4, CH])
        den_sum = s.sb("den_sum", [P, 3, CH])
        inv = s.sb("inv", [P, CH])
        w_o = s.sb("w_o", [P, KD, D])
        b_o = s.sb("b_o", [P, KD])
        spread = s.sb("spread", [P, NCH, KD, P])
        pair_sum = s.sb("pair_sum", [P, 2, 2, KD, CH])
        num_sum = s.sb("num_sum", [P, 2, KD, CH])
        y = s.sb("y", [P, 2, KD, CH])
        ps = s.ps("ps", [P, 2, KD, CH])
        ps_inv = s.ps("ps_inv", [P, 2, KD, CH])
        w_loaded = s.sem("w_loaded")
        den_loaded = s.sem("den_loaded")
        loaded = [s.sem(f"loaded{u}") for u in range(2)]
        den_step = s.sem("den_step")
        inv_ready = s.sem("inv_ready")
        inv_spread = s.sem("inv_spread")
        paired = s.sem("paired")
        paired_dve = s.sem("paired_dve")
        summed = s.sem("summed")
        y_ready = s.sem("y_ready")
        ps_ready = s.sem("ps_ready")
        added = s.sem("added")
        with s.block() as block:
            @block.sync
            def _(sp):
                sp.dma_start(den[:], den_dram.rearrange("g h (c t) -> (h c) g t", c=NCH)).then_inc(den_loaded, 16)
                sp.dma_start(spread[:], w["head_spread"]).then_inc(w_loaded, 16)
                sp.dma_start(w_o[:], w["wo"]).then_inc(w_loaded, 16)
                sp.dma_start(b_o[:], w["bo"]).then_inc(w_loaded, 16)
                for c in range(NCH):
                    if c >= 2:
                        sp.wait_ge(paired, c - 1)
                        sp.wait_ge(paired_dve, c - 1)
                    for g in range(4):
                        sp.dma_start(num[:, c % 2, g], num_dram[g, :, c * CH:(c + 1) * CH].rearrange(
                            "(k p) t -> p k t", p=P)).then_inc(loaded[c % 2], 16)

            @block.gpsimd
            def _(pool):
                for c in range(NCH):
                    pool.wait_ge(loaded[c % 2], 64 * (c // 2 + 1))
                    if c >= 2:
                        pool.wait_ge(summed, c - 1)
                    pool.tensor_tensor(pair_sum[:, c % 2, 0], num[:, c % 2, 0], num[:, c % 2, 1],
                                       ALU.add).then_inc(paired, 1)

            @block.vector
            def _(dve):
                dve.wait_ge(den_loaded, 16)
                dve.tensor_tensor(den_sum[:, 0], den[:, 0], den[:, 1], ALU.add)
                dve.tensor_tensor(den_sum[:, 1], den[:, 2], den[:, 3], ALU.add).then_inc(den_step, 1)
                dve.wait_ge(den_step, 1)
                dve.tensor_tensor(den_sum[:, 2], den_sum[:, 0], den_sum[:, 1], ALU.add).then_inc(den_step, 1)
                dve.wait_ge(den_step, 2)
                dve.reciprocal(inv[:], den_sum[:, 2]).then_inc(inv_ready, 1)

                def add(c):
                    dve.wait_ge(ps_ready, c + 1)
                    for m in range(KD):
                        x_c = x_t[:, m, c * CH:(c + 1) * CH]
                        a = dve.scalar_tensor_tensor(out=x_c, in0=ps[:, c % 2, m, :], scalar=b_o[:, m:m + 1],
                                                     in1=x_c, op0=ALU.add, op1=ALU.add)
                    a.then_inc(added, 1)

                for c in range(NCH):
                    u = c % 2
                    dve.wait_ge(loaded[u], 64 * (c // 2 + 1))
                    if c >= 2:
                        dve.wait_ge(summed, c - 1)
                    dve.tensor_tensor(pair_sum[:, u, 1], num[:, u, 2], num[:, u, 3], ALU.add).then_inc(paired_dve, 1)
                    dve.wait_ge(paired, c + 1)
                    dve.wait_ge(paired_dve, c + 1)
                    if c >= 2:
                        dve.wait_ge(y_ready, c - 1)
                    dve.tensor_tensor(num_sum[:, u], pair_sum[:, u, 0], pair_sum[:, u, 1], ALU.add).then_inc(summed, 1)
                    dve.wait_ge(summed, c + 1)
                    dve.wait_ge(inv_spread, c + 1)
                    if c >= 2:
                        dve.wait_ge(ps_ready, c - 1)
                    dve.tensor_tensor(y[:, u], num_sum[:, u], ps_inv[:, u], ALU.mult).then_inc(y_ready, 1)
                    if c >= 1:
                        if c == 1:
                            dve.wait_ge(w_loaded, 48)
                        add(c - 1)
                add(NCH - 1)

            @block.tensor
            def _(pe):
                pe.wait_ge(w_loaded, 48)
                pe.wait_ge(inv_ready, 1)

                def spread_inv(c):
                    if c >= 2:
                        pe.wait_ge(y_ready, c - 1)
                    for k in range(KD):
                        mm = pe.matmul(ps_inv[:, c % 2, k, :], spread[:, c, k, :], inv[:], start=True, stop=True)
                    mm.then_inc(inv_spread, 1)

                spread_inv(0)
                for c in range(NCH):
                    if c + 1 < NCH:
                        spread_inv(c + 1)
                    pe.wait_ge(y_ready, c + 1)
                    if c >= 2:
                        pe.wait_ge(added, c - 1)
                    for m in range(KD):
                        for k in range(KD):
                            mm = pe.matmul(ps[:, c % 2, m, :], w_o[:, k, m * P:(m + 1) * P], y[:, c % 2, k, :],
                                           start=(k == 0), stop=(k == KD - 1))
                    mm.then_inc(ps_ready, 1)


def route(nc, w, xn, w8, slot8, tile_expert, xs_dram):
    with Stage(nc, "route") as s:
        w_gate = s.sb("w_gate", [P, KD, EXPERTS])
        cst = s.sb("cst", [P, 2 * P])
        earlier = s.sb("earlier", [P, P], BF16)
        ones = s.sb("ones", [P, P], BF16)
        logits = s.sb("logits", [P, TT, EXPERTS])
        top = s.sb("top", [P, TT, TOPK])
        replaced = s.sb("replaced", [P, TT, EXPERTS])
        chosen = s.sb("chosen", [P, TT, EXPERTS], BF16)
        ex = s.sb("ex", [P, TT, EXPERTS])
        weight = s.sb("weight", [P, TT, EXPERTS])
        z_sum = s.sb("z_sum", [P, 3, TT])
        before = s.sb("before", [P, TT + 1, EXPERTS])
        pos = s.sb("pos", [P, TT, EXPERTS])
        equal = s.sb("equal", [P, TT, EXPERTS])
        top_pos = s.sb("top_pos", [P, TT, TOPK])
        cols = s.sb("cols", [P, 6, EXPERTS])
        count_i = s.sb("count_i", [P, 2, EXPERTS], I32)
        te = s.sb("te", [P, 4])
        te_i = s.sb("te_i", [P, 2], I32)
        pa = s.ps("pa", [P, TT, EXPERTS])
        pb = s.ps("pb", [P, TT, EXPERTS])
        ps_row = pb[:].rearrange("p (b i) e -> p b (i e)", b=4)
        ident = s.sb("ident", [P, P])
        row = s.sb("row", [P, 4, D])
        loaded = s.sem("loaded")
        const_ready = s.sem("const_ready")
        logits_ready = s.sem("logits_ready")
        copied = s.sem("copied")
        top_ready = s.sem("top_ready")
        repl_ready = s.sem("repl_ready")
        chosen_ready = s.sem("chosen_ready")
        shifted = s.sem("shifted")
        exp_ready = s.sem("exp_ready")
        ranks_ready = s.sem("ranks_ready")
        step_done = s.sem("step_done")
        te_ready = s.sem("te_ready")
        pb_read = s.sem("pb_read")
        slots_ready = s.sem("slots_ready")
        turned = s.sem("turned")
        row_ready = s.sem("row_ready")
        scattered = [s.sem(f"scattered{u}") for u in range(4)]
        stored = s.sem("stored")
        with s.block() as block:
            @block.sync
            def _(sp):
                sp.dma_start(w_gate[:], w["gate0"]).then_inc(loaded, 16)
                sp.dma_start(cst[:], w["route_consts"]).then_inc(loaded, 16)
                sp.dma_start(ident[:], w["ident"]).then_inc(loaded, 16)
                sp.wait_ge(te_ready, 1)
                for a in range(2):
                    sp.dma_start(tile_expert[0, a * P:(a + 1) * P].rearrange("(p o) -> p o", o=1),
                                 te_i[:, a:a + 1]).then_inc(stored, 16)
                sp.wait_ge(stored, 32)

            @block.tensor
            def _(pe):
                pe.wait_ge(loaded, 48)
                for i in range(TT):
                    for k in range(KD):
                        mm = pe.matmul(pa[:, i, :], xn[:, k, i * P:(i + 1) * P], w_gate[:, k, :],
                                       start=(k == 0), stop=(k == KD - 1))
                    mm.then_inc(logits_ready, 1)
                pe.wait_ge(copied, 4)
                pe.wait_ge(const_ready, 2)
                for b in range(4):
                    tiles = slice(8 * b, 8 * b + 8)
                    pe.wait_ge(chosen_ready, 1)
                    pe.matmul(pa[:, tiles, :], earlier[:], chosen[:, tiles, :], start=True, stop=True)
                    pe.matmul(pb[:, tiles, :], ones[:], chosen[:, tiles, :], start=True,
                              stop=True).then_inc(ranks_ready, 1)
                pe.wait_ge(pb_read, 1)
                for i in range(TT):
                    if i >= 4:
                        pe.wait_ge(row_ready, i - 3)
                    for k in range(KD):
                        mm = pe.transpose(ps_row[:, i % 4, k * P:(k + 1) * P], xn[:, k, i * P:(i + 1) * P], ident[:])
                    mm.then_inc(turned, 1)

            @block.scalar
            def _(act):
                for b in range(4):
                    act.wait_ge(logits_ready, 8 * b + 8)
                    act.activation(logits[:, 8 * b:8 * b + 8, :], pa[:, 8 * b:8 * b + 8, :],
                                   ACT.Copy).then_inc(copied, 1)
                act.wait_ge(shifted, 1)
                act.activation(ex[:], replaced[:], ACT.Exp).then_inc(exp_ready, 1)
                for i in range(TT):
                    act.wait_ge(turned, i + 1)
                    if i >= 4:
                        act.wait_ge(scattered[i % 4], 16 * TOPK * (i // 4))
                    act.activation(row[:, i % 4, :], ps_row[:, i % 4, 0:D], ACT.Copy).then_inc(row_ready, 1)

            @block.gpsimd
            def _(pool):
                pool.wait_ge(slots_ready, 1)
                for i in range(TT):
                    pool.wait_ge(row_ready, i + 1)
                    for j in range(TOPK):
                        pool.indirect_dma_start(out=xs_dram, out_offset=bass.IndirectOffsetOnAxis(slot8[:, i, j:j + 1], 0),
                                                in_=row[:, i % 4, :], in_offset=None).then_inc(scattered[i % 4], 16)
                for u in range(4):
                    pool.wait_ge(scattered[u], 16 * TOPK * (TT // 4))

            @block.vector
            def _(dve):
                steps = [0]

                def step(ins):
                    steps[0] += 1
                    ins.then_inc(step_done, 1)
                    dve.wait_ge(step_done, steps[0])

                dve.memset(ones[:], 1.0).then_inc(const_ready, 1)
                dve.wait_ge(loaded, 48)
                dve.tensor_copy(earlier[:], cst[:, 0:P]).then_inc(const_ready, 1)
                for i in range(TT):
                    dve.wait_ge(copied, i // 8 + 1)
                    dve.max(top[:, i, :], logits[:, i, :]).then_inc(top_ready, 1)
                for i in range(TT):
                    dve.wait_ge(top_ready, i + 1)
                    dve.match_replace(replaced[:, i, :], top[:, i, :], logits[:, i, :], -3.0e38).then_inc(repl_ready, 1)
                dve.wait_ge(repl_ready, TT)
                dve.tensor_tensor(chosen[:], logits[:], replaced[:], ALU.not_equal).then_inc(chosen_ready, 1)
                dve.wait_ge(chosen_ready, 1)
                dve.tensor_tensor(replaced[:], logits[:], top[:, :, 0:1].to_broadcast([P, TT, EXPERTS]),
                                  ALU.subtract).then_inc(shifted, 1)

                step(dve.memset(before[:, 0, :], 0.0))
                for i in range(TT):
                    dve.wait_ge(ranks_ready, i // 8 + 1)
                    step(dve.tensor_tensor(before[:, i + 1, :], before[:, i, :], pb[:, i, :], ALU.add))
                dve.nop().then_inc(pb_read, 1)
                step(dve.tensor_scalar(count_i[:, 0, :], before[:, TT, :], float(SLOT_TILE - 1), None, ALU.add))
                step(dve.tensor_scalar(count_i[:, 1, :], count_i[:, 0, :], SLOT_TILE.bit_length() - 1, None,
                                       ALU.arith_shift_right))
                step(dve.tensor_copy(cols[:, 0, :], count_i[:, 1, :]))
                step(dve.memset(cols[:, 1, :], 1.0))
                step(dve.tensor_tensor_scan(cols[:, 2, :], cols[:, 1, :], cols[:, 0, :], 0.0, ALU.mult, ALU.add))
                step(dve.tensor_tensor(cols[:, 3, :], cols[:, 2, :], cols[:, 0, :], ALU.subtract))
                step(dve.tensor_scalar(cols[:, 4, :], cols[:, 3, :], float(SLOT_TILE), 1.0, ALU.mult, ALU.add))
                step(dve.tensor_tensor(pos[:], pa[:], before[:, 0:TT, :], ALU.add))
                step(dve.tensor_tensor(pos[:], pos[:], cols[:, 4:5, :].to_broadcast([P, TT, EXPERTS]), ALU.add))
                step(dve.tensor_tensor(pos[:], pos[:], chosen[:], ALU.mult))
                for i in range(TT):
                    ins = dve.max(top_pos[:, i, :], pos[:, i, :])
                step(ins)
                step(dve.tensor_scalar(slot8[:], top_pos[:], -1.0, None, ALU.add))
                dve.nop().then_inc(slots_ready, 1)

                for a in range(2):
                    step(dve.tensor_scalar(te[:, 2 * a:2 * a + 1], cst[:, P:P + 1], float(a * P), None, ALU.add))
                    step(dve.tensor_scalar(cols[:, 5, :], cols[:, 2, :], te[:, 2 * a:2 * a + 1], None, ALU.is_le))
                    step(dve.tensor_reduce(te[:, 2 * a + 1:2 * a + 2], cols[:, 5, :], AX_X, ALU.add))
                    step(dve.tensor_scalar(te_i[:, a:a + 1], te[:, 2 * a + 1:2 * a + 2], float(EXPERTS - 1), None,
                                           ALU.min))
                dve.nop().then_inc(te_ready, 1)

                dve.wait_ge(exp_ready, 1)
                dve.tensor_reduce(z_sum[:, 0, :], ex[:], AX_X, ALU.add)
                step(dve.tensor_tensor(weight[:], ex[:], chosen[:], ALU.mult))
                step(dve.tensor_reduce(z_sum[:, 1, :], weight[:], AX_X, ALU.add))
                step(dve.scalar_tensor_tensor(out=z_sum[:, 2, :], in0=z_sum[:, 0, :], scalar=1e-20,
                                              in1=z_sum[:, 1, :], op0=ALU.mult, op1=ALU.add))
                step(dve.reciprocal(z_sum[:, 0, :], z_sum[:, 2, :]))
                step(dve.tensor_tensor(weight[:], weight[:],
                                       z_sum[:, 0, :].unsqueeze(2).to_broadcast([P, TT, EXPERTS]), ALU.mult))
                for j in range(TOPK):
                    step(dve.tensor_tensor(equal[:], pos[:], top_pos[:, :, j:j + 1].to_broadcast([P, TT, EXPERTS]),
                                           ALU.is_equal))
                    step(dve.tensor_tensor(equal[:], equal[:], weight[:], ALU.mult))
                    step(dve.tensor_reduce(w8[:, :, j], equal[:], AX_X, ALU.add))


def experts(nc, w, xs_dram, ys_dram, tile_expert):
    GU = 3 * P
    RING = 4
    with Stage(nc, "exp") as s:
        te_row = s.sb("te_row", [1, 2 * P], I32)
        ident = s.sb("ident", [P, P])
        w_gu = s.sb("w_gu", [P, RING, KD * GU + D])
        w_dn = s.sb("w_dn", [P, RING, D])
        rows = s.sb("rows", [P, RING, 2, D])
        x_k = s.sb("x_k", [P, 2, KD, SLOT_TILE])
        act_a = s.sb("act_a", [P, 2, SLOT_TILE])
        act_b = s.sb("act_b", [P, 2, SLOT_TILE])
        h_a = s.sb("h_a", [P, 2, SLOT_TILE])
        h_b = s.sb("h_b", [P, 2, SLOT_TILE])
        y = s.sb("y", [P, RING, 2, D])
        ps_x = s.ps("ps_x", [P, 2, KD, SLOT_TILE])
        ps_a = s.ps("ps_a", [P, 2, 2, SLOT_TILE])
        ps_b = s.ps("ps_b", [P, 2, CH])
        ps_y = s.ps("ps_y", [P, 2, 2, D])
        te_loaded = s.sem("te_loaded")
        sp_passed = s.sem("sp_passed")
        w_loaded = [s.sem(f"w_loaded{v}") for v in range(RING)]
        rows_loaded = [s.sem(f"rows_loaded{v}") for v in range(RING)]
        turned = s.sem("turned")
        x_ready = s.sem("x_ready")
        gu_ready = s.sem("gu_ready")
        silu_ready = s.sem("silu_ready")
        h_ready = s.sem("h_ready")
        y_ready = s.sem("y_ready")
        y_copied = s.sem("y_copied")
        y_stored = [s.sem(f"y_stored{v}") for v in range(RING)]

        def turn(pe, t, v):
            u = v % 2
            pe.wait_ge(rows_loaded[v], (t - v) * 4 + 16)
            pe.wait_ge(x_ready, t + 3)
            for k in range(KD):
                for a in range(2):
                    mm = pe.transpose(ps_x[:, u, k, a * P:(a + 1) * P], rows[:, v, a, k * P:(k + 1) * P], ident[:])
            mm.then_inc(turned, 1)

        def gate_up(pe, t, v):
            u = v % 2
            pe.wait_ge(w_loaded[v], (t - v) * 8 + 32)
            pe.wait_ge(x_ready, t + 5)
            pe.wait_ge(h_ready, t + 1)
            outs = [ps_a[:, u, 0, :], ps_a[:, u, 1, :], ps_b[:, u, 0:SLOT_TILE]]
            for m in range(3):
                for k in range(KD):
                    at = k * GU + m * P
                    mm = pe.matmul(outs[m], w_gu[:, v, at:at + P], x_k[:, u, k, :], start=(k == 0), stop=(k == KD - 1))
            mm.then_inc(gu_ready, 1)

        def down(pe, t, v):
            u = v % 2
            pe.wait_ge(h_ready, t + 3)
            pe.wait_ge(y_copied, t + 1)
            for a in range(2):
                c = slice(a * P, (a + 1) * P)
                pe.matmul(ps_y[:, u, a, :], h_a[:, u, c], w_gu[:, v, KD * GU:KD * GU + D], start=True, stop=False)
                mm = pe.matmul(ps_y[:, u, a, :], h_b[64:P, u, c], w_dn[64:P, v, :], start=False, stop=True)
            mm.then_inc(y_ready, 1)

        def silu(act, t, v):
            u = v % 2
            act.wait_ge(gu_ready, t + 3)
            act.wait_ge(h_ready, t + 1)
            act.activation(act_a[:, u, :], ps_a[:, u, 0, :], ACT.Silu)
            act.activation(act_b[64:P, u, :], ps_b[0:64, u, 0:SLOT_TILE], ACT.Silu).then_inc(silu_ready, 1)

        def copy_y(act, t, v):
            act.wait_ge(y_ready, t + 5)
            act.wait_ge(y_stored[v], (t - v) * 4 + 16)
            act.activation(y[:, v], ps_y[:, v % 2], ACT.Copy).then_inc(y_copied, 1)

        def store_y(act, t, v):
            act.wait_ge(y_copied, t + 3)
            act.dma_start(ys_dram[ds(t * SLOT_TILE, SLOT_TILE), :].rearrange("(a p) d -> p a d", p=P),
                          y[:, v]).then_inc(y_stored[v], 16)

        def copy_x(dve, t, v):
            u = v % 2
            dve.wait_ge(turned, t + 1)
            dve.wait_ge(gu_ready, t + 1)
            dve.tensor_copy(x_k[:, u], ps_x[:, u]).then_inc(x_ready, 1)

        def product(dve, t, v):
            u = v % 2
            dve.wait_ge(silu_ready, t + 1)
            dve.wait_ge(y_ready, t + 3)
            dve.tensor_tensor(h_a[:, u, :], act_a[:, u, :], ps_a[:, u, 1, :], ALU.mult)
            dve.tensor_tensor(h_b[64:P, u, :], act_b[64:P, u, :], ps_b[64:P, u, 0:SLOT_TILE],
                              ALU.mult).then_inc(h_ready, 1)

        with s.block() as block:
            @block.sync
            def _(sp):
                for v in range(RING):
                    sp.nop().then_inc(y_stored[v], 16)
                sp.dma_start(ident[:], w["consts"][:, 0:P]).then_inc(te_loaded, 16)
                sp.dma_start(te_row[:], tile_expert).then_inc(te_loaded, 16)
                sp.wait_ge(te_loaded, 32)
                with sp.Fori(0, SLOT_TILES // RING) as four:
                    for v in range(RING):
                        t = four * RING + v
                        at = sp.snap(t * SLOT_TILE)
                        e = sp.value_load(te_row[0:1, ds(t, 1)], min_val=0, max_val=EXPERTS - 1)
                        sp.wait_ge(x_ready, t + 1)
                        sp.nop().then_inc(sp_passed, 1)
                        sp.dma_start(rows[:, v], xs_dram[ds(at, SLOT_TILE), :].rearrange(
                            "(a p) d -> p a d", p=P)).then_inc(rows_loaded[v], 16)
                        sp.wait_ge(y_ready, t + 1)
                        sp.nop().then_inc(sp_passed, 1)
                        sp.dma_start(w_gu[:, v, :], w["gate_up"][ds(e, 1)].rearrange("o p n -> p (o n)")).then_inc(w_loaded[v], 16)
                        sp.dma_start(w_dn[64:P, v, :], w["down"][ds(e, 1)].rearrange("o p n -> p (o n)")).then_inc(w_loaded[v], 16)

            @block.scalar
            def _(act):
                silu(act, 0, 0)
                silu(act, 1, 1)
                copy_y(act, 0, 0)
                silu(act, 2, 2)
                copy_y(act, 1, 1)
                store_y(act, 0, 0)
                silu(act, 3, 3)
                copy_y(act, 2, 2)
                store_y(act, 1, 1)
                with act.Fori(1, SLOT_TILES // RING) as four:
                    for v in range(RING):
                        t = four * RING + v
                        silu(act, t, v)
                        copy_y(act, t - 1, (v - 1) % RING)
                        store_y(act, t - 2, (v - 2) % RING)
                last = SLOT_TILES - 1
                copy_y(act, last, RING - 1)
                store_y(act, last - 1, RING - 2)
                store_y(act, last, RING - 1)
                for v in range(RING):
                    act.wait_ge(y_stored[v], 16 * (SLOT_TILES // RING) + 16)

            @block.vector
            def _(dve):
                dve.nop().then_inc(x_ready, 4)
                dve.nop().then_inc(h_ready, 2)
                dve.nop().then_inc(y_copied, 2)
                copy_x(dve, 0, 0)
                for t in range(1, RING):
                    copy_x(dve, t, t)
                    product(dve, t - 1, t - 1)
                with dve.Fori(1, SLOT_TILES // RING) as four:
                    for v in range(RING):
                        t = four * RING + v
                        copy_x(dve, t, v)
                        product(dve, t - 1, (v - 1) % RING)
                product(dve, SLOT_TILES - 1, RING - 1)

            @block.tensor
            def _(pe):
                pe.nop().then_inc(gu_ready, 2)
                pe.nop().then_inc(y_ready, 4)
                pe.wait_ge(te_loaded, 32)

                turn(pe, 0, 0)
                turn(pe, 1, 1)
                gate_up(pe, 0, 0)
                for t in range(2, RING):
                    turn(pe, t, t)
                    gate_up(pe, t - 1, t - 1)
                    down(pe, t - 2, t - 2)
                with pe.Fori(1, SLOT_TILES // RING) as four:
                    for v in range(RING):
                        t = four * RING + v
                        turn(pe, t, v)
                        gate_up(pe, t - 1, (v - 1) % RING)
                        down(pe, t - 2, (v - 2) % RING)
                last = SLOT_TILES - 1
                gate_up(pe, last, RING - 1)
                down(pe, last - 1, RING - 2)
                down(pe, last, RING - 1)


def combine_scan_in(nc, w, ys_dram, w8, slot8, x_t, xs_t, z_dram):
    LEAD = TAPS - 1
    TPC = CH // P
    with Stage(nc, "csin") as s:
        ident = s.sb("ident", [P, P])
        got = s.sb("got", [P, TPC, TOPK, D])
        diag = s.sb("diag", [P, 2, TOPK, P])
        ones = s.sb("ones", [P, P])
        eps = s.sb("eps", [P, 1])
        xn = s.sb("xn", [P, 2, KD, CH])
        sq = s.sb("sq", [P, KD, CH])
        std = s.sb("std", [P, CH])
        rstd = s.sb("rstd", [P, CH])
        w_in = s.sb("w_in", [P, KD, 2 * DI])
        taps = s.sb("taps", [P, KI, TAPS])
        bias = s.sb("bias", [P, KI])
        xp = s.sb("xp", [P, 2, KI, LEAD + CH])
        conv = s.sb("conv", [P, 2, TAPS, CH])
        zb = s.sb("zb", [P, 2, CH])
        ps = s.ps("ps", [P, 2, CH])
        mean = s.ps("mean", [P, CH])
        var = s.ps("var", [P, CH])
        ps_x = s.ps("ps_x", [P, 2, CH])
        ps_z = s.ps("ps_z", [P, 2, CH])
        loaded = s.sem("loaded")
        const_ready = s.sem("const_ready")
        gathered = [s.sem(f"gathered{u}") for u in range(TPC)]
        diag_ready = s.sem("diag_ready")
        sum_ready = s.sem("sum_ready")
        added = s.sem("added")
        mean_ready = s.sem("mean_ready")
        centered = s.sem("centered")
        squared = s.sem("squared")
        var_ready = s.sem("var_ready")
        std_ready = s.sem("std_ready")
        rstd_ready = s.sem("rstd_ready")
        normed = s.sem("normed")
        x_ready = s.sem("x_ready")
        x_copied = s.sem("x_copied")
        lead_ready = s.sem("lead_ready")
        zeroed = s.sem("zeroed")
        conv_step = s.sem("conv_step")
        conv_done = s.sem("conv_done")
        xs_done = s.sem("xs_done")
        z_ready = s.sem("z_ready")
        z_done = s.sem("z_done")
        z_stored = [s.sem(f"z_stored{u}") for u in range(2)]
        sp_passed = s.sem("sp_passed")

        def chunks(eng, body):
            with eng.Fori(0, NCH // 2 - 1) as pair:
                for u in range(2):
                    body(pair * 2 + u, u, True)
            body(NCH - 2, 0, True)
            body(NCH - 1, 1, False)

        with s.block() as block:
            @block.gpsimd
            def _(pool):
                pool.memset(ones[:], 1.0 / D).then_inc(const_ready, 1)
                pool.memset(eps[:], EPS).then_inc(const_ready, 1)
                for i in range(TT):
                    if i >= TPC:
                        pool.wait_ge(sum_ready, i - TPC + 3)
                    for j in range(TOPK):
                        pool.indirect_dma_start(out=got[:, i % TPC, j, :], out_offset=None, in_=ys_dram,
                                                in_offset=bass.IndirectOffsetOnAxis(slot8[:, i, j:j + 1], 0)
                                                ).then_inc(gathered[i % TPC], 16)

            @block.sync
            def _(sp):
                sp.nop().then_inc(z_stored[0], 16)
                sp.nop().then_inc(z_stored[1], 16)
                for dst, src in ((ident[:], w["ident"]), (w_in[:], w["w_in"]), (taps[:], w["taps"]),
                                 (bias[:], w["conv_b"])):
                    sp.dma_start(dst, src).then_inc(loaded, 16)
                with sp.Fori(0, NCH) as c:
                    for m in range(KI):
                        sp.wait_ge(z_done, c * KI + (m + 3))
                        sp.nop().then_inc(sp_passed, 1)
                        sp.dma_start(z_dram[m, :, ds(c * CH, CH)], zb[:, m % 2, :]).then_inc(z_stored[m % 2], 16)
                for u in range(2):
                    sp.wait_ge(z_stored[u], 16 * (2 * NCH + 1))

            @block.tensor
            def _(pe):
                pe.nop().then_inc(sum_ready, 2)
                pe.nop().then_inc(z_ready, 8)
                pe.wait_ge(loaded, 64)
                pe.wait_ge(const_ready, 2)

                def combine(c, a):
                    i = c * TPC + a
                    pe.wait_ge(diag_ready, i + 1)
                    pe.wait_ge(gathered[a], c * (16 * TOPK) + 16 * TOPK)
                    pe.wait_ge(added, i + 1)
                    for m in range(KD):
                        for j in range(TOPK):
                            mm = pe.matmul(ps[:, a % 2, m * P:(m + 1) * P], got[:, a, j, m * P:(m + 1) * P],
                                           diag[:, a % 2, j, :], start=(j == 0), stop=(j == TOPK - 1))
                    mm.then_inc(sum_ready, 1)

                def project(c, u, half, m):
                    out, ready, free = [(ps_x, x_ready, x_copied), (ps_z, z_ready, z_done)][half]
                    pe.wait_ge(free, c * KI + (m + 1))
                    for k in range(KD):
                        at = half * DI + m * P
                        mm = pe.matmul(out[:, m % 2, :], w_in[:, k, at:at + P], xn[:, u, k, :],
                                       start=(k == 0), stop=(k == KD - 1))
                    mm.then_inc(ready, 1)

                def body(c, u, more):
                    pe.wait_ge(added, c * TPC + (TPC + 2))
                    pe.wait_ge(centered, c + 1)
                    for k in range(KD):
                        mm = pe.matmul(mean[:], ones[:], x_t[:, k, ds(c * CH, CH)], start=(k == 0), stop=(k == KD - 1))
                    mm.then_inc(mean_ready, 1)
                    if more:
                        combine(c + 1, 0)
                    pe.wait_ge(squared, c + 1)
                    pe.wait_ge(std_ready, c + 1)
                    for k in range(KD):
                        mm = pe.matmul(var[:], ones[:], sq[:, k, :], start=(k == 0), stop=(k == KD - 1))
                    mm.then_inc(var_ready, 1)
                    if more:
                        combine(c + 1, 1)
                    pe.wait_ge(normed, c + 2)
                    project(c, u, 0, 0)
                    project(c, u, 0, 1)
                    if more:
                        combine(c + 1, 2)
                    project(c, u, 0, 2)
                    project(c, u, 0, 3)
                    if more:
                        combine(c + 1, 3)
                    for m in range(KI):
                        project(c, u, 1, m)

                for a in range(TPC):
                    combine(0, a)
                chunks(pe, body)

            @block.scalar
            def _(act):
                act.nop().then_inc(std_ready, 1)
                act.nop().then_inc(x_copied, 2)
                act.nop().then_inc(xs_done, 2)
                act.nop().then_inc(z_done, 2)
                act.wait_ge(const_ready, 2)
                act.wait_ge(zeroed, 1)
                act.nop().then_inc(lead_ready, KI)
                act.wait_ge(loaded, 64)
                with act.Fori(0, NCH // 2) as pair:
                    for u in range(2):
                        c = pair * 2 + u
                        act.wait_ge(centered, c + 2)
                        act.activation(sq[:], xn[:, u], ACT.Square).then_inc(squared, 1)
                        act.wait_ge(var_ready, c + 1)
                        act.wait_ge(rstd_ready, c + 1)
                        act.activation(std[:], var[:], ACT.Sqrt, bias=eps[:]).then_inc(std_ready, 1)
                        for m in range(KI):
                            n = c * KI + m
                            act.wait_ge(x_ready, n + 1)
                            act.wait_ge(conv_done, n + 1)
                            act.activation(xp[:, u, m, LEAD:], ps_x[:, m % 2, :], ACT.Copy).then_inc(x_copied, 1)
                            act.wait_ge(conv_done, n + 5)
                            act.wait_ge(x_copied, n + 3)
                            act.activation(xp[:, 1 - u, m, 0:LEAD], xp[:, u, m, CH:], ACT.Copy).then_inc(lead_ready, 1)
                        for m in range(KI):
                            n = c * KI + m
                            act.wait_ge(conv_done, n + 9)
                            act.activation(xs_t[:, m, ds(c * CH, CH)], conv[:, m % 2, TAPS - 1, :], ACT.Silu,
                                           bias=bias[:, m:m + 1]).then_inc(xs_done, 1)
                        for m in range(KI):
                            n = c * KI + m
                            act.wait_ge(z_ready, n + 9)
                            act.wait_ge(z_stored[m % 2], c * 32 + (16 * (m // 2) + 16))
                            act.activation(zb[:, m % 2, :], ps_z[:, m % 2, :], ACT.Silu).then_inc(z_done, 1)

            @block.vector
            def _(dve):
                dve.nop().then_inc(added, 2)
                dve.nop().then_inc(centered, 1)
                dve.nop().then_inc(rstd_ready, 1)
                dve.nop().then_inc(normed, 1)
                dve.nop().then_inc(conv_done, 8)
                dve.memset(xp[:, 0, :, 0:LEAD], 0.0).then_inc(zeroed, 1)
                dve.wait_ge(loaded, 64)

                def make_diag(i, a):
                    dve.wait_ge(sum_ready, i + 1)
                    w_i = w8[:, ds(i, 1), :].rearrange("p o j -> p (o j)")
                    dve.tensor_tensor(diag[:, a % 2], ident[:].unsqueeze(1).to_broadcast([P, TOPK, P]),
                                      w_i.unsqueeze(2).to_broadcast([P, TOPK, P]), ALU.mult).then_inc(diag_ready, 1)

                def add(i, a):
                    dve.wait_ge(sum_ready, i + 3)
                    x_i = x_t[:, :, ds(i * P, P)]
                    dve.tensor_tensor(x_i, x_i, ps[:, a % 2, 0:KD * P].rearrange("p (m t) -> p m t", m=KD),
                                      ALU.add).then_inc(added, 1)

                def normalise(c, u):
                    dve.wait_ge(mean_ready, c + 1)
                    dve.wait_ge(z_ready, c * KI + KI)
                    for k in range(KD):
                        ins = dve.tensor_tensor(xn[:, u, k, :], x_t[:, k, ds(c * CH, CH)], mean[:], ALU.subtract)
                    ins.then_inc(centered, 1)
                    dve.wait_ge(std_ready, c + 2)
                    dve.wait_ge(normed, c + 1)
                    dve.reciprocal(rstd[:], std[:]).then_inc(rstd_ready, 1)
                    dve.wait_ge(rstd_ready, c + 2)
                    dve.tensor_tensor(xn[:, u], xn[:, u], rstd[:].unsqueeze(1).to_broadcast([P, KD, CH]),
                                      ALU.mult).then_inc(normed, 1)

                def convolve(c, u, m):
                    n = c * KI + m
                    dve.wait_ge(x_copied, n + 3)
                    dve.wait_ge(lead_ready, n + 1)
                    dve.wait_ge(xs_done, n + 1)
                    cv = conv[:, m % 2]
                    dve.tensor_scalar(cv[:, 0, :], xp[:, u, m, 0:CH], taps[:, m, 0:1], None,
                                      ALU.mult).then_inc(conv_step, 1)
                    for k in range(1, TAPS):
                        dve.wait_ge(conv_step, n * (TAPS - 1) + k)
                        ins = dve.scalar_tensor_tensor(out=cv[:, k, :], in0=xp[:, u, m, k:k + CH],
                                                       scalar=taps[:, m, k:k + 1], in1=cv[:, k - 1, :],
                                                       op0=ALU.mult, op1=ALU.add)
                        ins.then_inc(conv_step if k < TAPS - 1 else conv_done, 1)

                def body(c, u, more):
                    i = c * TPC + TPC
                    if more:
                        make_diag(i, 0)
                        make_diag(i + 1, 1)
                    normalise(c, u)
                    if more:
                        add(i, 0)
                        make_diag(i + 2, 2)
                        add(i + 1, 1)
                        make_diag(i + 3, 3)
                    convolve(c, u, 0)
                    convolve(c, u, 1)
                    if more:
                        add(i + 2, 2)
                    convolve(c, u, 2)
                    convolve(c, u, 3)
                    if more:
                        add(i + 3, 3)

                for a in range(TPC):
                    make_diag(a, a)
                    if a >= 1:
                        add(a - 1, a - 1)
                add(TPC - 1, TPC - 1)
                chunks(dve, body)


def scan_rates(nc, w, xs_t, dt_dram, bc_dram):
    with Stage(nc, "rate") as s:
        w_dt = s.sb("w_dt", [P, KI, DI])
        w_bc = s.sb("w_bc", [P, KI, P])
        bias = s.sb("bias", [P, KI])
        mag = s.sb("mag", [P, 2, KI, CH])
        pos = s.sb("pos", [P, 2, KI, CH])
        dt = s.sb("dt", [P, 2, KI, CH])
        bc = s.sb("bc", [P, 2, CH])
        bc_rest = s.sb("bc_rest", [BC, CH])
        bc_part = s.sb("bc_part", [BC, 2, 3, CH], BF16)
        ps = s.ps("ps", [P, KI, CH])
        ps_bc = s.ps("ps_bc", [P, 2, CH])
        loaded = s.sem("loaded")
        ps_ready = s.sem("ps_ready")
        abs_done = s.sem("abs_done")
        exp_done = s.sem("exp_done")
        ln_done = s.sem("ln_done")
        pos_done = s.sem("pos_done")
        dt_done = s.sem("dt_done")
        bc_ready = s.sem("bc_ready")
        bc_copied = s.sem("bc_copied")
        bc_step = s.sem("bc_step")
        bc_split = s.sem("bc_split")
        pool_passed = s.sem("pool_passed")
        stored = [s.sem(f"stored{u}") for u in range(2)]
        bc_stored = [s.sem(f"bc_stored{u}") for u in range(2)]
        sp_passed = s.sem("sp_passed")
        with s.block() as block:
            @block.sync
            def _(sp):
                for u in range(2):
                    sp.nop().then_inc(stored[u], 16)
                    sp.nop().then_inc(bc_stored[u], 48)
                sp.dma_start(w_dt[:], w["w_dt"]).then_inc(loaded, 16)
                sp.dma_start(w_bc[:], w["w_bc"]).then_inc(loaded, 16)
                sp.dma_start(bias[:], w["dt_b"]).then_inc(loaded, 16)
                with sp.Fori(0, NCH // 2) as pair:
                    for u in range(2):
                        c = pair * 2 + u
                        sp.wait_ge(bc_split, c + 3)
                        sp.nop().then_inc(sp_passed, 1)
                        for a in range(3):
                            rows = slice(a * 2 * NS, (a + 1) * 2 * NS)
                            sp.dma_start(bc_dram[rows, ds(c * CH, CH)], bc_part[rows, u, a, :]).then_inc(bc_stored[u], 16)
                        sp.wait_ge(dt_done, c + 3)
                        sp.nop().then_inc(sp_passed, 1)
                        sp.dma_start(dt_dram[:, :, ds(c * CH, CH)], dt[:, u]).then_inc(stored[u], 16)
                for u in range(2):
                    sp.wait_ge(stored[u], 8 * NCH + 16)
                    sp.wait_ge(bc_stored[u], 24 * NCH + 48)

            @block.gpsimd
            def _(pool):
                pool.nop().then_inc(bc_split, 2)
                with pool.Fori(0, NCH // 2) as pair:
                    for u in range(2):
                        c = pair * 2 + u
                        high, middle, low = (bc_part[:, u, a, :] for a in range(3))
                        pool.wait_ge(bc_copied, c + 3)
                        pool.wait_ge(bc_stored[u], pair * 48 + 48)
                        pool.wait_ge(bc_split, c + 2)
                        pool.nop().then_inc(pool_passed, 1)
                        pool.tensor_copy(high, bc[0:BC, u, :]).then_inc(bc_step, 1)
                        pool.wait_ge(bc_step, c * 3 + 1)
                        pool.tensor_tensor(bc_rest[:], bc[0:BC, u, :], high, ALU.subtract).then_inc(bc_step, 1)
                        pool.wait_ge(bc_step, c * 3 + 2)
                        pool.nop().then_inc(pool_passed, 1)
                        pool.tensor_copy(middle, bc_rest[:]).then_inc(bc_step, 1)
                        pool.wait_ge(bc_step, c * 3 + 3)
                        pool.tensor_tensor(low, bc_rest[:], middle, ALU.subtract).then_inc(bc_split, 1)

            @block.tensor
            def _(pe):
                pe.wait_ge(loaded, 48)
                with pe.Fori(0, NCH // 2) as pair:
                    for u in range(2):
                        c = pair * 2 + u
                        pe.wait_ge(bc_copied, c + 1)
                        for k in range(KI):
                            mm = pe.matmul(ps_bc[:, u, :], w_bc[:, k, :], xs_t[:, k, ds(c * CH, CH)],
                                           start=(k == 0), stop=(k == KI - 1))
                        mm.then_inc(bc_ready, 1)
                        for m in range(KI):
                            pe.wait_ge(pos_done, c * KI + (m + 1))
                            for k in range(KI):
                                mm = pe.matmul(ps[:, m, :], w_dt[:, k, m * P:(m + 1) * P], xs_t[:, k, ds(c * CH, CH)],
                                               start=(k == 0), stop=(k == KI - 1))
                            mm.then_inc(ps_ready, 1)

            @block.scalar
            def _(act):
                act.nop().then_inc(bc_copied, 2)
                act.wait_ge(loaded, 48)
                with act.Fori(0, NCH // 2) as pair:
                    for u in range(2):
                        c = pair * 2 + u
                        act.wait_ge(bc_ready, c + 1)
                        act.wait_ge(bc_split, c + 1)
                        act.activation(bc[:, u, :], ps_bc[:, u, :], ACT.Copy).then_inc(bc_copied, 1)
                        act.wait_ge(dt_done, c + 1)
                        for m in range(KI):
                            act.wait_ge(ps_ready, c * KI + (m + 1))
                            act.activation(mag[:, u, m, :], ps[:, m, :], ACT.Abs, bias=bias[:, m:m + 1]).then_inc(abs_done, 1)
                        act.wait_ge(abs_done, c * KI + 4)
                        act.activation(mag[:, u], mag[:, u], ACT.Exp, scale=-1.0).then_inc(exp_done, 1)
                        act.wait_ge(exp_done, c + 1)
                        act.activation(mag[:, u], mag[:, u], ACT.Ln, bias=1.0).then_inc(ln_done, 1)

            @block.vector
            def _(dve):
                dve.nop().then_inc(pos_done, 4)
                dve.nop().then_inc(dt_done, 2)
                dve.wait_ge(loaded, 48)
                with dve.Fori(0, NCH // 2) as pair:
                    for u in range(2):
                        c = pair * 2 + u
                        for m in range(KI):
                            dve.wait_ge(abs_done, c * KI + (m + 1))
                            dve.tensor_scalar(pos[:, u, m, :], ps[:, m, :], bias[:, m:m + 1], 0.0, ALU.add,
                                              ALU.max).then_inc(pos_done, 1)
                        dve.wait_ge(pos_done, c * KI + 8)
                        dve.wait_ge(ln_done, c + 1)
                        dve.wait_ge(stored[u], pair * 16 + 16)
                        dve.tensor_tensor(dt[:, u], pos[:, u], mag[:, u], ALU.add).then_inc(dt_done, 1)


def scan(nc, w, xs_t, dt_dram, bc_dram):
    with Stage(nc, "scan") as s:
        ident = s.sb("ident", [P, P])
        sel = s.sb("sel", [BC, 2, NS, P], BF16)
        a_col = s.sb("a_col", [P, KI, NS])
        a_log = s.sb("a_log", [P, KI, NS])
        skip = s.sb("skip", [P, KI])
        dt = s.sb("dt", [P, 2, KI, CH])
        bc = s.sb("bc", [BC, 2, CH], BF16)
        dtx = s.sb("dtx", [P, 2, KI, CH])
        decay = s.sb("decay", [P, 2, KI, CH])
        b_row = s.sb("b_row", [P, 2, CH])
        gain = s.sb("gain", [P, 2, KI, CH])
        h = s.sb("h", [P, 2, KI, CH])
        ch = s.sb("ch", [P, 2, KI, CH])
        last = s.sb("last", [P, NS, KI])
        ps_b = s.ps("ps_b", [P, 2, CH])
        ps_c = s.ps("ps_c", [P, 2, CH])
        ps_y = s.ps("ps_y", [P, KI, CH])
        sel_f32 = ch[0:BC].rearrange("p u k t -> p (u k t)").rearrange("p (a n m) -> p a n m", a=2, n=NS)
        w_loaded = s.sem("w_loaded")
        sel_ready = s.sem("sel_ready")
        zeroed = s.sem("zeroed")
        a_exp = s.sem("a_exp")
        a_ready = s.sem("a_ready")
        loaded = [s.sem(f"loaded{u}") for u in range(2)]
        b_spread = s.sem("b_spread")
        b_copied = s.sem("b_copied")
        c_spread = s.sem("c_spread")
        dtx_ready = s.sem("dtx_ready")
        gain_ready = s.sem("gain_ready")
        decay_ready = s.sem("decay_ready")
        h_ready = s.sem("h_ready")
        last_ready = s.sem("last_ready")
        ch_ready = s.sem("ch_ready")
        y_added = s.sem("y_added")
        y_done = s.sem("y_done")
        sp_passed = s.sem("sp_passed")

        def chunks(eng, body):
            for c in range(2):
                body(c, c, c == 0, True)
            with eng.Fori(1, NCH // 2 - 1) as pair:
                for u in range(2):
                    body(pair * 2 + u, u, False, True)
            for c in range(NCH - 2, NCH):
                body(c, c % 2, False, c < NCH - 1)

        def inputs_count(c, u):
            return (c - u) * 16 + 32

        with s.block() as block:
            @block.gpsimd
            def _(pool):
                pool.nop().then_inc(gain_ready, 2)

                def body(c, u, first, more):
                    pool.wait_ge(dtx_ready, c + 1)
                    for n in range(NS):
                        g = c * NS + n
                        pool.wait_ge(b_copied, g + 3)
                        pool.wait_ge(h_ready, g + 1)
                        pool.tensor_tensor(gain[:, n % 2], dtx[:, u],
                                           b_row[:, n % 2, :].unsqueeze(1).to_broadcast([P, KI, CH]),
                                           ALU.mult).then_inc(gain_ready, 1)

                chunks(pool, body)

            @block.sync
            def _(sp):
                for dst, name in ((ident[:], "ident"), (sel_f32, "sel"), (a_log[:], "a_log"), (skip[:], "skip")):
                    sp.dma_start(dst, w[name]).then_inc(w_loaded, 16)
                with sp.Fori(0, NCH // 2) as pair:
                    for u in range(2):
                        c = pair * 2 + u
                        sp.wait_ge(y_done, c + 1)
                        sp.nop().then_inc(sp_passed, 1)
                        sp.dma_start(bc[:, u, :], bc_dram[:, ds(c * CH, CH)]).then_inc(loaded[u], 16)
                        sp.dma_start(dt[:, u], dt_dram[:, :, ds(c * CH, CH)]).then_inc(loaded[u], 16)

            @block.tensor
            def _(pe):
                pe.nop().then_inc(y_added, 2)
                pe.wait_ge(w_loaded, 64)
                pe.wait_ge(sel_ready, 1)

                def spread_b(c, u, n):
                    pe.wait_ge(b_copied, c * NS + (n + 1))
                    pe.matmul(ps_b[:, n % 2, :], sel[:, 0, n, :], bc[:, u, :], start=True,
                              stop=True).then_inc(b_spread, 1)

                def spread_c(u, n):
                    pe.matmul(ps_c[:, n % 2, :], sel[:, 1, n, :], bc[:, u, :], start=True,
                              stop=True).then_inc(c_spread, 1)

                def add(c, n):
                    pe.wait_ge(ch_ready, c * NS + (n + 3))
                    if n == 0:
                        pe.wait_ge(y_done, c + 2)
                    for m in range(KI):
                        mm = pe.matmul(ps_y[:, m, :], ident[:], ch[:, n % 2, m, :], start=(n == 0), stop=(n == NS - 1))
                    mm.then_inc(y_added, 1)

                def body(c, u, first, more):
                    if first:
                        pe.wait_ge(loaded[0], inputs_count(0, 0))
                        for n in range(3):
                            spread_b(0, 0, n)
                        pe.wait_ge(ch_ready, 1)
                        spread_c(0, 0)
                    for n in range(NS):
                        if n + 3 == NS and more:
                            pe.wait_ge(loaded[1 - u], inputs_count(c + 1, 1 - u))
                        if n + 1 < NS or more:
                            pe.wait_ge(ch_ready, c * NS + (n + 2))
                        if n + 3 < NS:
                            spread_b(c, u, n + 3)
                        elif more:
                            spread_b(c + 1, 1 - u, n + 3 - NS)
                        if n + 1 < NS:
                            spread_c(u, n + 1)
                        elif more:
                            spread_c(1 - u, 0)
                        add(c, n)

                chunks(pe, body)

            @block.scalar
            def _(act):
                act.nop().then_inc(b_copied, 2)
                act.wait_ge(w_loaded, 64)
                act.activation(a_col[:], a_log[:], ACT.Exp).then_inc(a_exp, 1)
                act.wait_ge(a_ready, 1)
                act.wait_ge(zeroed, 1)
                act.nop().then_inc(last_ready, NS)

                def copy_b(c, n):
                    g = c * NS + n
                    act.wait_ge(b_spread, g + 1)
                    act.wait_ge(gain_ready, g + 1)
                    act.activation(b_row[:, n % 2, :], ps_b[:, n % 2, :], ACT.Copy).then_inc(b_copied, 1)

                def keep_last(c, n):
                    act.wait_ge(h_ready, c * NS + (n + 3))
                    act.activation(last[:, n, :], h[:, n % 2, :, CH - 1], ACT.Copy).then_inc(last_ready, 1)

                def body(c, u, first, more):
                    if first:
                        copy_b(0, 0)
                    act.wait_ge(loaded[u], inputs_count(c, u))
                    for n in range(NS):
                        act.wait_ge(h_ready, c * NS + (n + 1))
                        if n >= 2:
                            keep_last(c, n - 2)
                        elif not first:
                            keep_last(c - 1, NS - 2 + n)
                        for m in range(KI):
                            a = act.activation(decay[:, n % 2, m, :], dt[:, u, m, :], ACT.Exp,
                                               scale=a_col[:, m, n:n + 1])
                        a.then_inc(decay_ready, 1)
                        if n + 1 < NS:
                            copy_b(c, n + 1)
                        elif more:
                            copy_b(c + 1, 0)

                chunks(act, body)

            @block.vector
            def _(dve):
                dve.nop().then_inc(h_ready, 2)
                dve.nop().then_inc(ch_ready, 2)
                dve.nop().then_inc(y_done, 2)
                dve.memset(last[:], 0.0).then_inc(zeroed, 1)
                dve.wait_ge(w_loaded, 64)
                dve.tensor_copy(sel[:], sel_f32).then_inc(sel_ready, 1)
                dve.wait_ge(a_exp, 1)
                dve.tensor_scalar(a_col[:], a_col[:], -1.0, None, ALU.mult).then_inc(a_ready, 1)

                def times_x(c, u):
                    dve.wait_ge(loaded[u], inputs_count(c, u))
                    dve.tensor_tensor(dtx[:, u], dt[:, u], xs_t[:, :, ds(c * CH, CH)], ALU.mult).then_inc(dtx_ready, 1)

                def times_c(c, n):
                    g = c * NS + n
                    dve.wait_ge(c_spread, g + 1)
                    dve.wait_ge(h_ready, g + 3)
                    dve.wait_ge(y_added, g + 1)
                    dve.tensor_tensor(ch[:, n % 2], h[:, n % 2],
                                      ps_c[:, n % 2, :].unsqueeze(1).to_broadcast([P, KI, CH]), ALU.mult).then_inc(ch_ready, 1)

                def finish(c):
                    dve.wait_ge(y_added, c * NS + (NS + 2))
                    for m in range(KI):
                        x_c = xs_t[:, m, ds(c * CH, CH)]
                        st = dve.scalar_tensor_tensor(out=x_c, in0=x_c, scalar=skip[:, m:m + 1], in1=ps_y[:, m, :],
                                                      op0=ALU.mult, op1=ALU.add)
                    st.then_inc(y_done, 1)

                def body(c, u, first, more):
                    if first:
                        times_x(0, 0)
                    for n in range(NS):
                        g = c * NS + n
                        dve.wait_ge(decay_ready, g + 1)
                        dve.wait_ge(gain_ready, g + 3)
                        dve.wait_ge(last_ready, g + 15)
                        dve.wait_ge(ch_ready, g + 1)
                        for m in range(KI):
                            sc = dve.tensor_tensor_scan(h[:, n % 2, m, :], decay[:, n % 2, m, :], gain[:, n % 2, m, :],
                                                        last[:, n, m:m + 1], ALU.mult, ALU.add)
                        sc.then_inc(h_ready, 1)
                        if n >= 1:
                            times_c(c, n - 1)
                        elif not first:
                            times_c(c - 1, NS - 1)
                        if n == 1 and not first:
                            finish(c - 1)
                        if n == NS // 2 and more:
                            times_x(c + 1, 1 - u)
                    if not more:
                        times_c(c, NS - 1)
                        finish(c)

                chunks(dve, body)


def scan_out(nc, w, y_t, z_dram, x_t):
    with Stage(nc, "sout") as s:
        w_out = s.sb("w_out", [P, KI, D])
        z = s.sb("z", [P, 2, KI, CH])
        ps = s.ps("ps", [P, 4, CH])
        w_loaded = s.sem("w_loaded")
        loaded = [s.sem(f"loaded{u}") for u in range(2)]
        gated = s.sem("gated")
        ps_ready = s.sem("ps_ready")
        added = s.sem("added")
        sp_passed = s.sem("sp_passed")
        with s.block() as block:
            @block.sync
            def _(sp):
                sp.dma_start(w_out[:], w["w_out"]).then_inc(w_loaded, 16)
                with sp.Fori(0, NCH // 2) as pair:
                    for u in range(2):
                        c = pair * 2 + u
                        sp.wait_ge(gated, c + 1)
                        sp.nop().then_inc(sp_passed, 1)
                        sp.dma_start(z[:, u], z_dram[:, :, ds(c * CH, CH)].rearrange("k p t -> p k t")).then_inc(loaded[u], 16)

            @block.tensor
            def _(pe):
                pe.wait_ge(w_loaded, 16)
                with pe.Fori(0, NCH // 2) as pair:
                    for u in range(2):
                        c = pair * 2 + u
                        pe.wait_ge(gated, c + 3)
                        for m in range(KD):
                            pe.wait_ge(added, c * KD + (m + 1))
                            for k in range(KI):
                                mm = pe.matmul(ps[:, 2 * u + m, :], w_out[:, k, m * P:(m + 1) * P],
                                               y_t[:, k, ds(c * CH, CH)], start=(k == 0), stop=(k == KI - 1))
                            mm.then_inc(ps_ready, 1)

            @block.vector
            def _(dve):
                dve.nop().then_inc(gated, 2)
                dve.nop().then_inc(added, 4)

                def gate(c, u):
                    y_c = y_t[:, :, ds(c * CH, CH)]
                    dve.wait_ge(loaded[u], (c - u) * 8 + 16)
                    dve.tensor_tensor(y_c, y_c, z[:, u], ALU.mult).then_inc(gated, 1)

                def add(c, u):
                    for m in range(KD):
                        dve.wait_ge(ps_ready, c * KD + (m + 1))
                        dve.tensor_tensor(x_t[:, m, ds(c * CH, CH)], x_t[:, m, ds(c * CH, CH)], ps[:, 2 * u + m, :],
                                          ALU.add).then_inc(added, 1)

                gate(0, 0)
                gate(1, 1)
                add(0, 0)
                with dve.Fori(1, NCH // 2) as pair:
                    for u in range(2):
                        gate(pair * 2 + u, u)
                        add(pair * 2 + (u - 1), 1 - u)
                add(NCH - 1, 1)


def scan_layer(nc, w, xs_t, z_dram, x_t):
    dt_dram = nc.dram_tensor("dt_rates", [P, KI, T], F32).ap()
    bc_dram = nc.dram_tensor("bc_rows", [BC, T], BF16).ap()
    scan_rates(nc, w, xs_t, dt_dram, bc_dram)
    scan(nc, w, xs_t, dt_dram, bc_dram)
    scan_out(nc, w, xs_t, z_dram, x_t)


def small_gates(nc, w, xn, gate_rows):
    with Stage(nc, "sgate") as s:
        w_gate = s.sb("w_gate", [P, KD, E2])
        ident = s.sb("ident", [P, P])
        logits = s.sb("logits", [P, TT, E2])
        rank = s.sb("rank", [P, TT, E2])
        over = s.sb("over", [P, TT, E2])
        shifted = s.sb("shifted", [P, TT, E2])
        ex = s.sb("ex", [P, TT, E2])
        cols = s.sb("cols", [P, 3, TT])
        ps = s.ps("ps", [P, TT, E2])
        ps_t = s.ps("ps_t", [P, 2, CH])
        loaded = s.sem("loaded")
        logits_ready = s.sem("logits_ready")
        step_done = s.sem("step_done")
        shift_ready = s.sem("shift_ready")
        exp_ready = s.sem("exp_ready")
        gates_ready = s.sem("gates_ready")
        turned = s.sem("turned")
        copied = s.sem("copied")
        full = [P, TT, E2]
        with s.block() as block:
            @block.sync
            def _(sp):
                sp.dma_start(w_gate[:], w["gate1"]).then_inc(loaded, 16)
                sp.dma_start(ident[:], w["ident"]).then_inc(loaded, 16)

            @block.tensor
            def _(pe):
                pe.wait_ge(loaded, 32)
                for i in range(TT):
                    for k in range(KD):
                        mm = pe.matmul(ps[:, i, :], xn[:, k, i * P:(i + 1) * P], w_gate[:, k, :], start=(k == 0),
                                       stop=(k == KD - 1))
                mm.then_inc(logits_ready, 1)
                pe.wait_ge(gates_ready, 1)
                for c in range(NCH):
                    if c >= 2:
                        pe.wait_ge(copied, c - 1)
                    for a in range(4):
                        mm = pe.transpose(ps_t[0:E2, c % 2, a * P:(a + 1) * P], ex[:, 4 * c + a, :], ident[:])
                    mm.then_inc(turned, 1)

            @block.scalar
            def _(act):
                act.wait_ge(shift_ready, 1)
                act.activation(ex[:], shifted[:], ACT.Exp).then_inc(exp_ready, 1)
                for c in range(NCH):
                    act.wait_ge(turned, c + 1)
                    act.activation(gate_rows[0:E2, c * CH:(c + 1) * CH], ps_t[0:E2, c % 2, :], ACT.Copy).then_inc(copied, 1)

            @block.vector
            def _(dve):
                steps = [0]

                def step(ins):
                    steps[0] += 1
                    ins.then_inc(step_done, 1)
                    dve.wait_ge(step_done, steps[0])

                dve.wait_ge(logits_ready, 1)
                step(dve.tensor_copy(logits[:], ps[:]))
                step(dve.tensor_reduce(cols[:, 0, :], logits[:], AX_X, ALU.max))
                dve.tensor_tensor(shifted[:], logits[:], cols[:, 0, :].unsqueeze(2).to_broadcast(full),
                                  ALU.subtract).then_inc(shift_ready, 1)
                step(dve.memset(rank[:], 0.0))
                for e in range(E2):
                    if e > 0:
                        dve.tensor_tensor(over[:, :, 0:e], logits[:, :, e:e + 1].to_broadcast([P, TT, e]),
                                          logits[:, :, 0:e], ALU.is_gt)
                    if e < E2 - 1:
                        dve.tensor_tensor(over[:, :, e + 1:], logits[:, :, e:e + 1].to_broadcast([P, TT, E2 - 1 - e]),
                                          logits[:, :, e + 1:], ALU.is_ge)
                    step(dve.memset(over[:, :, e:e + 1], 0.0))
                    step(dve.tensor_tensor(rank[:], rank[:], over[:], ALU.add))
                step(dve.tensor_scalar(over[:], rank[:], 2.0, None, ALU.is_lt))
                dve.wait_ge(exp_ready, 1)
                step(dve.tensor_tensor(ex[:], ex[:], over[:], ALU.mult))
                step(dve.tensor_reduce(cols[:, 1, :], ex[:], AX_X, ALU.add))
                step(dve.reciprocal(cols[:, 2, :], cols[:, 1, :]))
                dve.tensor_tensor(ex[:], ex[:], cols[:, 2, :].unsqueeze(2).to_broadcast(full),
                                  ALU.mult).then_inc(gates_ready, 1)


def small_layer(nc, w, xn, gate_rows, x_t, out):
    with Stage(nc, "small") as s:
        w_u = s.sb("w_u", [P, KD, KR * P])
        w_v = s.sb("w_v", [P, KD, KR * P])
        w_o = s.sb("w_o", [P, KR, D])
        spread = s.sb("spread", [E2, KR, P])
        silu = s.sb("silu", [P, 2, CH])
        prod = s.sb("prod", [P, 2, CH])
        hid = s.sb("hid", [P, 2, KR, CH])
        ps_u = s.ps("ps_u", [P, 2, CH])
        ps_v = s.ps("ps_v", [P, 2, CH])
        ps_g = s.ps("ps_g", [P, 2, CH])
        ps_o = s.ps("ps_o", [P, KD, CH])
        loaded = s.sem("loaded")
        uv_ready = s.sem("uv_ready")
        silu_ready = s.sem("silu_ready")
        prod_ready = s.sem("prod_ready")
        hid_ready = s.sem("hid_ready")
        out_ready = s.sem("out_ready")
        added = s.sem("added")
        out_stored = s.sem("out_stored")
        with s.block() as block:
            @block.sync
            def _(sp):
                for dst, name in ((w_u[:], "w_u"), (w_v[:], "w_v"), (w_o[:], "w_o2"), (spread[:], "spread")):
                    sp.dma_start(dst, w[name]).then_inc(loaded, 16)
                for c in range(NCH):
                    cols = slice(c * CH, (c + 1) * CH)
                    sp.wait_ge(added, c + 2)
                    sp.dma_start(out[:, :, cols], x_t[:, :, cols]).then_inc(out_stored, 16)
                sp.wait_ge(out_stored, 16 * NCH)

            @block.tensor
            def _(pe):
                pe.nop().then_inc(out_ready, 2)
                pe.wait_ge(loaded, 64)
                with pe.Fori(0, NCH // 2) as pair:
                    for u in range(2):
                        c = pair * 2 + u
                        cols = ds(c * CH, CH)
                        for m in range(KR):
                            pe.wait_ge(hid_ready, c * KR + (m + 1))
                            f = slice(m * P, (m + 1) * P)
                            for ps, wt in ((ps_u, w_u), (ps_v, w_v)):
                                for k in range(KD):
                                    pe.matmul(ps[:, m % 2, :], wt[:, k, f], xn[:, k, cols], start=(k == 0),
                                              stop=(k == KD - 1))
                            pe.matmul(ps_g[:, m % 2, :], spread[:, m, :], gate_rows[0:E2, cols], start=True,
                                      stop=True).then_inc(uv_ready, 1)
                        pe.wait_ge(added, c + 1)
                        for k in range(KR):
                            pe.wait_ge(hid_ready, c * KR + (k + 3))
                            for m in range(KD):
                                mm = pe.matmul(ps_o[:, m, :], w_o[:, k, m * P:(m + 1) * P], hid[:, u, k, :],
                                               start=(k == 0), stop=(k == KR - 1))
                        mm.then_inc(out_ready, 1)

            @block.scalar
            def _(act):
                with act.Fori(0, NCH) as c:
                    for m in range(KR):
                        act.wait_ge(uv_ready, c * KR + (m + 1))
                        act.wait_ge(hid_ready, c * KR + (m + 1))
                        act.activation(silu[:, m % 2, :], ps_u[:, m % 2, :], ACT.Silu).then_inc(silu_ready, 1)

            @block.vector
            def _(dve):
                dve.nop().then_inc(hid_ready, 2)
                dve.nop().then_inc(added, 1)
                with dve.Fori(0, NCH // 2) as pair:
                    for u in range(2):
                        c = pair * 2 + u
                        dve.wait_ge(out_ready, c + 1)
                        for m in range(KR):
                            n = c * KR + m
                            dve.wait_ge(silu_ready, n + 1)
                            dve.tensor_tensor(prod[:, m % 2, :], silu[:, m % 2, :], ps_v[:, m % 2, :],
                                              ALU.mult).then_inc(prod_ready, 1)
                            dve.wait_ge(prod_ready, n + 1)
                            dve.tensor_tensor(hid[:, u, m, :], prod[:, m % 2, :], ps_g[:, m % 2, :],
                                              ALU.mult).then_inc(hid_ready, 1)
                        dve.wait_ge(out_ready, c + 3)
                        for m in range(KD):
                            cols = ds(c * CH, CH)
                            tt = dve.tensor_tensor(x_t[:, m, cols], x_t[:, m, cols], ps_o[:, m, :], ALU.add)
                        tt.then_inc(added, 1)


def small_experts(nc, w, xn, x_t, out):
    with nc.sbuf_tensor("gate_rows", [E2, T], F32) as gate_rows:
        small_gates(nc, w, xn, gate_rows)
        small_layer(nc, w, xn, gate_rows, x_t, out)


def build_program(nc, w, out):
    with ExitStack() as ctx:
        x_t = ctx.enter_context(nc.sbuf_tensor("x_t", [P, KD, T], F32))
        parts_dram = nc.dram_tensor("qk_parts", [2, 3, D, T], BF16).ap()
        num_dram = nc.dram_tensor("attn_num", [4, D, T], F32).ap()
        den_dram = nc.dram_tensor("attn_den", [4, HEADS, T], F32).ap()
        xs_dram = nc.dram_tensor("x_slots", [SLOTS, D], F32).ap()
        ys_dram = nc.dram_tensor("y_slots", [SLOTS, D], F32).ap()
        tile_expert = nc.dram_tensor("tile_expert", [1, P * 2], I32).ap()
        with nc.sbuf_tensor("v_all", [P, HEADS, TT, DH], F32) as v_all, nc.sbuf_tensor("xn1", [P, KD, T], F32) as xn:
            layernorm(nc, "ln1", w, x_t, xn, x_dram=w["x"])
            project_qk(nc, xn, w, parts_dram)
            attention(nc, w, xn, parts_dram, v_all, num_dram, den_dram, xs_dram)
        attention_out(nc, w, num_dram, den_dram, x_t)
        z_dram = nc.dram_tensor("z_gate", [KI, P, T], F32).ap()
        with nc.sbuf_tensor("xs_t", [P, KI, T], F32) as xs_t:
            with nc.sbuf_tensor("w8", [P, TT, TOPK], F32) as w8, nc.sbuf_tensor("slot8", [P, TT, TOPK], U32) as slot8:
                with nc.sbuf_tensor("xn2", [P, KD, T], F32) as xn:
                    layernorm(nc, "ln2", w, x_t, xn)
                    route(nc, w, xn, w8, slot8, tile_expert, xs_dram)
                experts(nc, w, xs_dram, ys_dram, tile_expert)
                combine_scan_in(nc, w, ys_dram, w8, slot8, x_t, xs_t, z_dram)
            scan_layer(nc, w, xs_t, z_dram, x_t)
        with nc.sbuf_tensor("xn4", [P, KD, T], F32) as xn:
            layernorm(nc, "ln4", w, x_t, xn)
            small_experts(nc, w, xn, x_t, out)


def _constants():
    ident = np.eye(P, dtype=np.float32)
    q, k = np.arange(P)[:, None], np.arange(P)[None, :]
    mask_q = np.where(k > q, NEG, 0.0).astype(np.float32)
    head_spread = np.zeros((HEADS, NCH, NCH, KD, P), np.float32)
    for f in range(D):
        for c in range(NCH):
            head_spread[f // DH, c, c, f // P, f % P] = 1.0
    mask_k = np.full((P, CH), NEG, np.float32)
    mask_k[:, 3 * P:] = np.where(np.arange(P)[:, None] > np.arange(P)[None, :], NEG, 0.0)
    consts = np.concatenate([ident, mask_q, mask_k], axis=1)
    j = np.arange(T, dtype=np.float32)[:, None]
    i = np.arange(DH // 2, dtype=np.float32)[None, :]
    theta = j * np.power(np.float32(10000.0), np.float32(-2.0) * i / np.float32(DH)).astype(np.float32)
    factor = (np.cos(theta) + np.sin(theta)).astype(np.float32)
    rope = np.ascontiguousarray(np.tile(factor.T, (P * 2 // DH, 1)))
    route_consts = np.zeros((P, 2 * P), np.float32)
    route_consts[:, :P] = np.arange(P)[:, None] < np.arange(P)[None, :]
    route_consts[:, P] = np.arange(P)
    sel = np.zeros((BC, 2, NS, P), np.float32)
    for n in range(NS):
        for part in range(3):
            sel[part * 2 * NS + n, 0, n] = 1.0
            sel[part * 2 * NS + NS + n, 1, n] = 1.0
    spread = np.zeros((E2, KR, P), np.float32)
    for e in range(E2):
        spread[e, e // 2, R2 * (e % 2):R2 * (e % 2) + R2] = 1.0
    to_row = np.zeros((P, 4, 4), np.float32)
    pick = np.zeros((4, 4, P), np.float32)
    for g in range(4):
        to_row[:, g, g] = 1.0 / D
        pick[g, g] = 1.0
    return {"to_row": to_row, "pick": pick, "consts": consts, "head_spread": head_spread.reshape(P, NCH, KD, P), "rope": rope, "route_consts": route_consts, "ident": ident, "sel": sel,
            "spread": spread}


def _by_rows(a):
    return np.ascontiguousarray(a.reshape(-1, P, a.shape[-1]).transpose(1, 0, 2))


def _column(a):
    return np.ascontiguousarray(a.reshape(-1, P).T)


def _layout(inp):
    f = lambda n: np.asarray(inp[n])
    L = dict(_constants())
    L["x"] = _by_rows(f("L0_attn_x")[0].T)
    for n in "qkvo":
        L[f"w{n}"] = _by_rows(f(f"L0_attn_W{n}").T)
    L["bq"], L["bk"], L["bo"] = (_column(f(f"L0_attn_b{n}")) for n in "qko")
    L["bv"] = np.ascontiguousarray(np.broadcast_to(f("L0_attn_bv"), (P, D)))
    L["gate0"] = _by_rows(f("L0_ffn_gate_w").T)
    gate, up, dn = (f(f"L0_ffn_w_{n}") for n in ("gate", "up", "down"))
    gu = np.concatenate([gate[:, :P], up[:, :P], gate[:, P:], up[:, P:]], axis=1).transpose(0, 2, 1)
    gu = gu.reshape(EXPERTS, KD, P, 3 * P).transpose(0, 2, 1, 3).reshape(EXPERTS, P, KD * 3 * P)
    dn = dn.transpose(0, 2, 1)
    L["gate_up"] = np.ascontiguousarray(np.concatenate([gu, dn[:, :P]], axis=2))
    L["down"] = np.ascontiguousarray(dn[:, P:])
    L["w_in"] = _by_rows(f("L1_attn_in_proj_w").T)
    L["taps"] = _by_rows(f("L1_attn_conv_w")[:, 0, :])
    L["conv_b"], L["dt_b"], L["skip"] = (_column(f(f"L1_attn_{n}")) for n in ("conv_b", "dt_b", "D_param"))
    L["w_dt"] = _by_rows(f("L1_attn_dt_w").T)
    bc = np.concatenate([f("L1_attn_B_proj_w"), f("L1_attn_C_proj_w")], axis=0).T
    L["w_bc"] = _by_rows(np.concatenate([bc] * (P // (2 * NS)), axis=1))
    L["a_log"] = _by_rows(f("L1_attn_A_log"))
    L["w_out"] = _by_rows(f("L1_attn_out_proj_w").T)
    L["gate1"] = _by_rows(f("L1_ffn_gate_w"))
    for n, name in (("u", "w_u"), ("v", "w_v")):
        L[name] = _by_rows(f(f"L1_ffn_W{n}").transpose(1, 0, 2).reshape(D, E2 * R2))
    L["w_o2"] = _by_rows(f("L1_ffn_Wo").reshape(E2 * R2, D))
    return L


def kernel(**inputs):
    import concourse.bacc as bacc
    from concourse.bass_utils import run_bass_kernel_spmd

    arrays = _layout(inputs)
    nc = bacc.Bacc("TRN2", target_bir_lowering=False, num_devices=1)
    w = {n: nc.dram_tensor(f"in_{n}", a.shape, mybir.dt.from_np(a.dtype), kind="ExternalInput").ap()
         for n, a in arrays.items()}
    out = nc.dram_tensor("out_x", (P, KD, T), F32, kind="ExternalOutput").ap()
    build_program(nc, w, out)
    r = run_bass_kernel_spmd(nc, [{f"in_{n}": a for n, a in arrays.items()}], core_ids=[0])
    got = r.results[0]["out_x"]
    return np.ascontiguousarray(got.transpose(2, 1, 0).reshape(1, T, D))
```
